# Optimizing a Trainium2 kernel written in Bass

```python
import numpy as np
import jax
import jax.numpy as jnp

def _softmax(x, axis=-1):
    return jax.nn.softmax(x, axis=axis)

def _gelu(x):
    return jax.nn.gelu(x, approximate=True)

def _silu(x):
    return jax.nn.silu(x)

def _sigmoid(x):
    return jax.nn.sigmoid(x)

def _layernorm(x, axis=-1, eps=1e-05):
    m = jnp.mean(x, axis=axis, keepdims=True)
    v = jnp.var(x, axis=axis, keepdims=True)
    return (x - m) / jnp.sqrt(v + eps)

def _scatter_add(tgt, idx, src, axis=0):
    return tgt.at[idx].add(src)

def _segment_sum(src, seg, n):
    return jax.ops.segment_sum(src, seg, n)
kernel_name = 'mk_gnn_preln_d1_gnn_r8_1ac952'

def setup_inputs(seed: int=0):
    np.random.seed(seed)
    _w = jnp.asarray

    def _rec_inputs():
        import jax
        import jax.numpy as jnp
        _gk = jax.random.key(seed)
        x = -8.776e-05 + 1 * jax.random.normal(jax.random.fold_in(_gk, 1), (6250, 128), jnp.float32)
        _s = jax.random.randint(jax.random.fold_in(_gk, 2), (100000,), 0, 6250, jnp.int32)
        _d = jax.random.randint(jax.random.fold_in(_gk, 3), (100000,), 0, 6250, jnp.int32)
        _loop = jnp.arange(6250, dtype=jnp.int32)
        src = jnp.concatenate([_s, _d, _loop])
        dst = jnp.concatenate([_d, _s, _loop])
        _o = jnp.argsort(dst, stable=True)
        src = src[_o]
        dst = dst[_o]
        edge_attr_50 = jax.random.uniform(jax.random.fold_in(_gk, 11), (206250, 50), jnp.float32, 0.0, 1)
        return (x, src, dst, edge_attr_50)
    x, src, dst, edge_attr_50 = _rec_inputs()

    def _L0_gnn_setup():
        import jax, jax.numpy as jnp
        import numpy as np
        N_NODES = 5000
        N_EDGES = 80000
        HIDDEN = 128
        FILTERS = 128
        NG = 50

        def _mlp_params(key, d_in, d_mid, d_out):
            k1, k2 = jax.random.split(key)
            s1 = 1.0 / np.sqrt(d_in)
            s2 = 1.0 / np.sqrt(d_mid)
            return (jax.random.uniform(k1, (d_in, d_mid), jnp.float32, -s1, s1), jnp.zeros((d_mid,), jnp.float32), jax.random.uniform(k2, (d_mid, d_out), jnp.float32, -s2, s2), jnp.zeros((d_out,), jnp.float32))
        key = jax.random.key(seed)
        ks = jax.random.split(key, 6)
        h = jax.random.normal(ks[0], (N_NODES, HIDDEN), jnp.float32)
        edge_index = jax.random.randint(ks[1], (2, N_EDGES), 0, N_NODES, jnp.int64)
        dist_feat = jax.random.uniform(ks[2], (N_EDGES, NG), jnp.float32)
        fw1, fb1, fw2, fb2 = _mlp_params(ks[3], NG, FILTERS, FILTERS)
        aw1, ab1, aw2, ab2 = _mlp_params(ks[4], HIDDEN, FILTERS, FILTERS)
        ow1, ob1, ow2, ob2 = _mlp_params(ks[5], FILTERS, HIDDEN, HIDDEN)
        return {'h': h, 'edge_index': edge_index, 'dist_feat': dist_feat, 'fw1': fw1, 'fb1': fb1, 'fw2': fw2, 'fb2': fb2, 'aw1': aw1, 'ab1': ab1, 'aw2': aw2, 'ab2': ab2, 'ow1': ow1, 'ob1': ob1, 'ow2': ow2, 'ob2': ob2}
    _L0_gnn_all = _L0_gnn_setup()
    _L0_gnn_in = {k: v for k, v in _L0_gnn_all.items() if k in ('fw1', 'fb1', 'fw2', 'fb2', 'aw1', 'ab1', 'aw2', 'ab2', 'ow1', 'ob1', 'ow2', 'ob2')}
    del _L0_gnn_all
    return {'x': x, 'src': src, 'dst': dst, 'edge_attr_50': edge_attr_50, 'L0_gnn_fw1': _L0_gnn_in['fw1'], 'L0_gnn_fb1': _L0_gnn_in['fb1'], 'L0_gnn_fw2': _L0_gnn_in['fw2'], 'L0_gnn_fb2': _L0_gnn_in['fb2'], 'L0_gnn_aw1': _L0_gnn_in['aw1'], 'L0_gnn_ab1': _L0_gnn_in['ab1'], 'L0_gnn_aw2': _L0_gnn_in['aw2'], 'L0_gnn_ab2': _L0_gnn_in['ab2'], 'L0_gnn_ow1': _L0_gnn_in['ow1'], 'L0_gnn_ob1': _L0_gnn_in['ob1'], 'L0_gnn_ow2': _L0_gnn_in['ow2'], 'L0_gnn_ob2': _L0_gnn_in['ob2']}

def reference(x, src, dst, edge_attr_50, L0_gnn_fw1, L0_gnn_fb1, L0_gnn_fw2, L0_gnn_fb2, L0_gnn_aw1, L0_gnn_ab1, L0_gnn_aw2, L0_gnn_ab2, L0_gnn_ow1, L0_gnn_ob1, L0_gnn_ow2, L0_gnn_ob2):
    import jax
    import jax.numpy as jnp

    def _L0_gnn_ref(h, edge_index, dist_feat, fw1, fb1, fw2, fb2, aw1, ab1, aw2, ab2, ow1, ob1, ow2, ob2):
        import jax, jax.numpy as jnp
        import numpy as np
        N_NODES = 5000
        N_EDGES = 80000
        HIDDEN = 128
        FILTERS = 128
        NG = 50

        def _mlp_params(key, d_in, d_mid, d_out):
            k1, k2 = jax.random.split(key)
            s1 = 1.0 / np.sqrt(d_in)
            s2 = 1.0 / np.sqrt(d_mid)
            return (jax.random.uniform(k1, (d_in, d_mid), jnp.float32, -s1, s1), jnp.zeros((d_mid,), jnp.float32), jax.random.uniform(k2, (d_mid, d_out), jnp.float32, -s2, s2), jnp.zeros((d_out,), jnp.float32))
        silu = jax.nn.silu
        src, dst = (edge_index[0], edge_index[1])
        W = silu(dist_feat @ fw1 + fb1) @ fw2 + fb2
        x = silu(h @ aw1 + ab1) @ aw2 + ab2
        msg = W * x[src]
        agg = jax.ops.segment_sum(msg, dst, num_segments=h.shape[0])
        out = silu(agg @ ow1 + ob1) @ ow2 + ob2
        return h + out
    edge_index = jnp.stack([src, dst])
    h = jnp.maximum(_layernorm(x, axis=-1), 0.0)
    x = x + _L0_gnn_ref(h, edge_index, edge_attr_50, L0_gnn_fw1, L0_gnn_fb1, L0_gnn_fw2, L0_gnn_fb2, L0_gnn_aw1, L0_gnn_ab1, L0_gnn_aw2, L0_gnn_ab2, L0_gnn_ow1, L0_gnn_ob1, L0_gnn_ow2, L0_gnn_ob2)
    return x

_drawn_inputs = setup_inputs


def setup_inputs(seed=0):
    import zlib

    import numpy as np

    out = dict(_drawn_inputs(seed))
    spreads = {'L0_gnn_fb1': (0.0, 0.605),
     'L0_gnn_fb2': (0.0, 0.1),
     'L0_gnn_ab1': (0.0, 0.63),
     'L0_gnn_ab2': (0.0, 0.1),
     'L0_gnn_ob1': (0.0, 0.413),
     'L0_gnn_ob2': (0.0, 0.1)}
    factors = {'edge_attr_50': 8.0}
    for name, (base, spread) in spreads.items():
        noise = np.random.default_rng([zlib.crc32(name.encode()), seed]).standard_normal(out[name].shape)
        drawn = base * np.exp(spread * noise) if base else spread * noise
        out[name] = jnp.asarray(drawn.astype(out[name].dtype))
    for name, factor in factors.items():
        out[name] = (out[name] * factor).astype(out[name].dtype)
    return out
```

```python
import numpy as np
import concourse.bass as bass
from concourse import mybir
from contextlib import ExitStack

P = 128
F = 128
NG = 50
N_NODES = 6250
N_EDGES = 206250
NODE_TILES = -(-N_NODES // P)
CH = 7
N_CHUNKS = NODE_TILES // CH
CHC = CH * P
TPG = 4
GC = TPG * P
EDGE_TILES = -(-N_EDGES // GC) * TPG
GROUPS = EDGE_TILES // TPG
SLOTS = 13
TURNS = GROUPS // SLOTS
SLOTS_A = 7
WIN = 64
RW = 512
R_WINDOWS = -(-(N_NODES + 1) // RW)
AGG = max(R_WINDOWS * RW, N_NODES + WIN)
EPS = 1e-5
assert NODE_TILES == N_CHUNKS * CH and GROUPS == TURNS * SLOTS


def ring_of(n, slots=SLOTS):
    return [s % n for s in range(slots - 1)] + [n]


def back(ring, s):
    return next(d for d in range(1, SLOTS + 1) if ring[(s - d) % SLOTS] == ring[s])


def gnn_layer(nc, x, src_t, dst_t, attr_t, fw1, fb1, fw2, fb2, aw1, ab1, aw2, ab2, ow1, ob1, ow2, ob2, out):
    f32, i32, bf16 = mybir.dt.float32, mybir.dt.int32, mybir.dt.bfloat16
    ALU, ACT, AX = mybir.AluOpType, mybir.ActivationFunctionType, mybir.AxisListType

    table = nc.dram_tensor("node_table", [NODE_TILES * P, F], f32).ap()
    x_tiles = x.rearrange("(t p) f -> p t f", p=P)
    out_tiles = out.rearrange("(t p) f -> p t f", p=P)
    table_tiles = table.rearrange("(t p) f -> p t f", p=P)

    with ExitStack() as ctx:
        def sb(name, shape, dt=f32):
            return ctx.enter_context(nc.sbuf_tensor(name, shape, dt))

        def sem(name):
            return ctx.enter_context(nc.semaphore(name))

        ident = sb("ident", [P, P])
        ones = sb("ones", [P, P])
        ones_b = sb("ones_b", [P, P], bf16)
        iota = sb("iota", [P, RW])
        w = {n: sb(n, [a.shape[0], F]) for n, a in
             (("fw1_s", fw1), ("fw2_s", fw2), ("aw1_s", aw1), ("aw2_s", aw2), ("ow1_s", ow1), ("ow2_s", ow2))}
        cols = sb("cols", [P, 3])
        rows = sb("rows", [P, 3, F])
        fb2_part = sb("fb2_part", [P, 3, F], bf16)
        fb2_rest = sb("fb2_rest", [P, 2, F])
        fb2_rows = sb("fb2_rows", [P, TPG, F], bf16)
        xs = sb("xs", [P, NODE_TILES, F])
        hs = sb("hs", [P, 2, CH, F])
        hT = sb("hT", [P, CHC])
        mid = sb("mid", [P, CHC])
        res = sb("res", [P, 2, CH, F])
        stats = sb("stats", [P, NODE_TILES, 6])
        moments = sb("moments", [P, 4, NODE_TILES])
        dst_i = sb("dst_i", [P, EDGE_TILES], i32)
        dst_f = sb("dst_f", [P, EDGE_TILES])
        rel = sb("rel", [P, EDGE_TILES])
        cover = sb("cover", [P, EDGE_TILES])
        n_cover = sb("n_cover", [P, 1])
        n_left = sb("n_left", [P, 1], i32)
        agg = sb("agg", [P, AGG])
        src_a = sb("src_a", [P, SLOTS_A * TPG], i32)
        src_b = sb("src_b", [P, (SLOTS - SLOTS_A) * TPG], i32)
        attr = sb("attr", [NG, SLOTS * GC])
        xg = sb("xg", [P, SLOTS, GC])
        hid = sb("hid", [P, 3, GC])
        msg = sb("msg", [P, 3, GC])
        onehot = sb("onehot", [P, 3, TPG, WIN])
        r_src = sb("r_src", [P, 1], i32)
        r_oh = sb("r_oh", [P, RW])

        banks = [ctx.enter_context(nc.psum_tensor(f"bank{i}", [P, 1024], f32)) for i in range(4)]
        bank = [banks[i // 2][:, 512 * (i % 2):512 * (i % 2) + 512] for i in range(8)]
        hid_ps, fil_ps, sum_ps = bank[0:3], bank[3:6], bank[6:8]
        tr_ps, l1_ps, l2_ps, misc_ps = banks[0], banks[1], banks[2], banks[3]

        s_wts, s_cols, s_rows, s_dst = sem("s_wts"), sem("s_cols"), sem("s_rows"), sem("s_dst")
        s_x = [sem(f"s_x{i}") for i in range(N_CHUNKS)]
        s_const, s_base = sem("s_const"), sem("s_base")
        s_pool, s_fb2 = sem("s_pool"), sem("s_fb2")
        s_dve, s_std, s_rstd = sem("s_dve"), sem("s_std"), sem("s_rstd")
        s_h, s_hx, s_tr, s_hT, s_l1, s_mid, s_l2, s_res = (sem(n) for n in
                                                     ("s_h", "s_hx", "s_tr", "s_hT", "s_l1", "s_mid", "s_l2", "s_res"))
        s_tab, s_rel = sem("s_tab"), sem("s_rel")
        attr_in, src_in = [sem("attr_in_a"), sem("attr_in_b")], [sem("src_in_a"), sem("src_in_b")]
        gathered = [sem(f"gathered{s}") for s in range(SLOTS)]
        taken, hid_sum, hid_done, fil_done, msg_done, win_done, win_added = (
            sem(n) for n in ("taken", "hid_sum", "hid_done", "fil_done", "msg_done", "win_done", "win_added"))
        s_cnt, s_left, s_agg = sem("s_cnt"), sem("s_left"), sem("s_agg")
        r_in, r_gat, r_l1, r_hid, r_fil, r_msg, r_one, r_win, r_add = (
            sem(n) for n in ("r_in", "r_gat", "r_l1", "r_hid", "r_fil", "r_msg", "r_one", "r_win", "r_add"))
        o_l1, o_mid, o_l2, o_res, o_out = (sem(n) for n in ("o_l1", "o_mid", "o_l2", "o_res", "o_out"))
        o_st = [sem("o_st0"), sem("o_st1")]

        ring_h, ring_w = ring_of(2), ring_of(1)
        ring_w = [s % 2 for s in range(SLOTS)]

        def done(turn, slot, d=0):
            return turn * SLOTS + (SLOTS + 1 + slot - d)

        def chunk(c, d=0):
            return c + (3 - d)

        block = ctx.enter_context(nc.Block())

        @block.sync
        def _(sp):
            for c in range(N_CHUNKS):
                sp.dma_start(xs[:, c * CH:(c + 1) * CH, :], x_tiles[:, c * CH:(c + 1) * CH, :]).then_inc(s_x[c], 16)
            part_cols = [(0, SLOTS_A), (SLOTS_A, SLOTS)]
            src_buf = [src_a, src_b]

            def load_src(turn, k):
                a, b = part_cols[k]
                sp.dma_start(src_buf[k][:, :], src_t[bass.ds(turn, 1), :, a * TPG:b * TPG].rearrange("o p j -> p (o j)")).then_inc(src_in[k], 16)

            def load_attr(turn, k):
                a, b = part_cols[k]
                sp.dma_start(attr[:, a * GC:b * GC],
                             attr_t[:, bass.ds(turn * (SLOTS * GC) + a * GC, (b - a) * GC)]).then_inc(attr_in[k], 16)

            for k in range(2):
                load_src(0, k)
            for k in range(2):
                load_attr(0, k)
            sp.sem_inc(s_tab, 32)
            with sp.Fori(0, N_CHUNKS) as c:
                sp.wait_ge(s_res, chunk(c))
                sp.dma_start(table_tiles[:, bass.ds(c * CH, CH), :], res[:, 0, :, :]).then_inc(s_tab, 16)
            with sp.Fori(1, TURNS) as turn:
                for k in range(2):
                    a, b = part_cols[k]
                    for s in range(a, b):
                        sp.wait_ge(gathered[s], turn * (16 * TPG))
                    load_src(turn, k)
                    sp.wait_ge(hid_sum, turn * SLOTS + b)
                    load_attr(turn, k)
            sp.wait_ge(s_left, 1)
            n = sp.value_load(n_left[0:1, 0:1], min_val=0, max_val=EDGE_TILES * P)
            with sp.If(n > 0):
                with sp.Fori(0, TURNS) as turn:
                    with sp.Fori(0, SLOTS * TPG) as j:
                        t = turn * (SLOTS * TPG) + j
                        sp.wait_ge(r_msg, t + 1)
                        sp.dma_start(r_src[:, :], src_t[bass.ds(turn, 1), :, bass.ds(j, 1)]
                                     .rearrange("o p j -> p (o j)"),
                                     allow_slow_non_contiguous=True).then_inc(r_in, 16)
                        sp.dma_start(attr[:, 0:P], attr_t[:, bass.ds(t * P, P)]).then_inc(r_in, 16)
            sp.sem_inc(o_out, 32)
            with sp.Fori(0, N_CHUNKS) as c:
                sp.wait_ge(o_res, chunk(c))
                sp.dma_start(out_tiles[:, bass.ds(c * CH, CH), :], res[:, 0, :, :]).then_inc(o_out, 16)
            sp.wait_ge(o_out, 16 * chunk(N_CHUNKS - 1))

        @block.gpsimd
        def _(pool):
            pool.memset(ident[:, :], 0.0).then_inc(s_pool, 1)
            pool.wait_ge(s_pool, 1)
            pool.affine_select(out=ident[:, :], in_=ident[:, :], compare_op=ALU.not_equal, fill=1.0, base=0,
                               pattern=[[-1, P]], channel_multiplier=1).then_inc(s_const, 1)
            pool.memset(ones[:, :], 1.0).then_inc(s_const, 1)
            pool.memset(ones_b[:, :], 1.0).then_inc(s_const, 1)
            pool.iota(iota[:, :], pattern=[[1, RW]], base=0, channel_multiplier=0,
                      allow_small_or_imprecise_dtypes=True).then_inc(s_const, 1)
            pool.memset(agg[:, :], 0.0).then_inc(s_const, 1)
            pool.memset(fb2_rows[:, :, :], 0.0).then_inc(s_pool, 1)
            pool.wait_ge(s_rows, 48)
            pool.tensor_copy(fb2_part[:, 0, :], rows[:, 0, :]).then_inc(s_pool, 1)
            pool.wait_ge(s_pool, 3)
            pool.tensor_tensor(fb2_rest[:, 0, :], rows[:, 0, :], fb2_part[:, 0, :], ALU.subtract).then_inc(s_pool, 1)
            pool.wait_ge(s_pool, 4)
            pool.tensor_copy(fb2_part[:, 1, :], fb2_rest[:, 0, :]).then_inc(s_pool, 1)
            pool.wait_ge(s_pool, 5)
            pool.tensor_tensor(fb2_rest[:, 1, :], fb2_rest[:, 0, :], fb2_part[:, 1, :],
                               ALU.subtract).then_inc(s_pool, 1)
            pool.wait_ge(s_pool, 6)
            pool.tensor_copy(fb2_part[:, 2, :], fb2_rest[:, 1, :]).then_inc(s_pool, 1)
            pool.wait_ge(s_pool, 7)
            for i in range(3):
                for j in range(TPG):
                    pool.tensor_copy(fb2_rows[32 * i:32 * i + 1, j, :],
                                     fb2_part[32 * i:32 * i + 1, i, :]).then_inc(s_fb2, 1)
            pool.wait_ge(s_fb2, 3 * TPG)
            pool.wait_ge(s_tab, 16 * chunk(N_CHUNKS - 1))
            with pool.Fori(0, TURNS) as turn:
                for s in range(SLOTS):
                    if s in (0, SLOTS_A):
                        pool.wait_ge(src_in[s // SLOTS_A], turn * 16 + 16)
                    pool.wait_ge(msg_done, done(turn, s, SLOTS))
                    pool.sem_inc(taken, 1)
                    idx, o = (src_a, s) if s < SLOTS_A else (src_b, s - SLOTS_A)
                    for j in range(TPG):
                        pool.indirect_dma_start(
                            xg[:, s, j * P:(j + 1) * P], None, table[:, :],
                            bass.IndirectOffsetOnAxis(ap=idx[:, o * TPG + j:o * TPG + j + 1], axis=0),
                        ).then_inc(gathered[s], 16)
            pool.wait_ge(s_left, 1)
            n = pool.value_load(n_left[0:1, 0:1], min_val=0, max_val=EDGE_TILES * P)
            with pool.If(n > 0):
                with pool.Fori(0, EDGE_TILES) as t:
                    pool.wait_ge(r_in, t * 32 + 32)
                    pool.wait_ge(r_msg, t + 1)
                    pool.sem_inc(taken, 1)
                    pool.indirect_dma_start(xg[:, 0, 0:P], None, table[:, :],
                                            bass.IndirectOffsetOnAxis(ap=r_src[:, 0:1], axis=0)).then_inc(r_gat, 16)

        @block.scalar
        def _(act):
            for name, a in (("aw1_s", aw1), ("aw2_s", aw2), ("fw1_s", fw1), ("fw2_s", fw2), ("ow1_s", ow1),
                            ("ow2_s", ow2)):
                act.dma_start(w[name][:, :], a).then_inc(s_wts, 16)
            for i, b in enumerate((fb2, ab2, ob2)):
                act.dma_start(rows[:, i, :], b.rearrange("(o f) -> o f", o=1).to_broadcast([P, F])).then_inc(s_rows, 16)
            for i, b in enumerate((fb1, ab1, ob1)):
                act.dma_start(cols[:, i:i + 1], b.rearrange("(f o) -> f o", o=1)).then_inc(s_cols, 16)
            act.dma_start(dst_i[:, :], dst_t).then_inc(s_dst, 16)
            act.wait_ge(s_std, 1)
            act.activation(moments[:, 2, :], moments[:, 2, :], ACT.Sqrt).then_inc(s_std, 1)

            def relu_ln(c, b):
                act.wait_ge(s_tr, chunk(c, 2))
                act.wait_ge(s_hx, chunk(c, 2))
                for j in range(CH):
                    t = c * CH + j
                    i = act.activation(hs[:, b, j, :], xs[:, bass.ds(t, 1), :].rearrange("p o f -> p (o f)"), ACT.Relu,
                                       bias=moments[:, 3, bass.ds(t, 1)], scale=moments[:, 2, bass.ds(t, 1)])
                i.then_inc(s_h, 1)

            def silu_mid(c, summed, used, bias, sem_out):
                act.wait_ge(summed, chunk(c))
                act.wait_ge(used, chunk(c, 1))
                act.activation(mid[:, :], l1_ps[:, 0:CHC], ACT.Silu, bias=cols[:, bias:bias + 1]).then_inc(sem_out, 1)

            act.sem_inc(s_h, 2)
            act.sem_inc(s_mid, 2)
            act.sem_inc(o_mid, 2)
            act.wait_ge(s_rstd, 1)
            act.wait_ge(s_cols, 48)
            relu_ln(0, 0)
            with act.Fori(0, (N_CHUNKS - 1) // 2) as pair:
                for k in range(2):
                    relu_ln(2 * pair + (k + 1), (k + 1) % 2)
                    silu_mid(2 * pair + k, s_l1, s_l2, 1, s_mid)
            silu_mid(N_CHUNKS - 1, s_l1, s_l2, 1, s_mid)

            act.sem_inc(hid_done, SLOTS)
            with act.Fori(0, TURNS) as turn:
                for s in range(SLOTS):
                    b = ring_h[s]
                    act.wait_ge(hid_sum, done(turn, s))
                    act.wait_ge(fil_done, done(turn, s, back(ring_h, s)))
                    act.activation(hid[:, b, :], hid_ps[b], ACT.Silu, bias=cols[:, 0:1]).then_inc(hid_done, 1)

            act.wait_ge(s_left, 1)
            n = act.value_load(n_left[0:1, 0:1], min_val=0, max_val=EDGE_TILES * P)
            with act.If(n > 0):
                with act.Fori(0, EDGE_TILES) as t:
                    act.wait_ge(r_l1, t + 1)
                    act.activation(hid[:, 0, 0:P], hid_ps[0][:, 0:P], ACT.Silu, bias=cols[:, 0:1]).then_inc(r_hid, 1)

            with act.Fori(0, N_CHUNKS) as c:
                silu_mid(c, o_l1, o_l2, 2, o_mid)

        @block.vector
        def _(dve):
            for c in range(N_CHUNKS):
                dve.wait_ge(s_x[c], 16)
                for t in range(c * CH, (c + 1) * CH):
                    i = dve.bn_stats(stats[:, t, :], xs[:, t, :])
            i.then_inc(s_dve, 1)
            dve.wait_ge(s_dve, 1)
            dve.tensor_tensor(moments[:, 0, :], stats[:, :, 1], stats[:, :, 4], ALU.add).then_inc(s_dve, 1)
            dve.tensor_tensor(moments[:, 1, :], stats[:, :, 1], stats[:, :, 4], ALU.subtract).then_inc(s_dve, 1)
            dve.tensor_tensor(moments[:, 2, :], stats[:, :, 2], stats[:, :, 5], ALU.add).then_inc(s_dve, 1)
            dve.wait_ge(s_dve, 4)
            dve.tensor_tensor(moments[:, 1, :], moments[:, 1, :], moments[:, 1, :], ALU.mult).then_inc(s_dve, 1)
            dve.wait_ge(s_dve, 5)
            dve.scalar_tensor_tensor(out=moments[:, 2, :], in0=moments[:, 1, :], scalar=F / 4.0,
                                     in1=moments[:, 2, :], op0=ALU.mult, op1=ALU.add).then_inc(s_dve, 1)
            dve.wait_ge(s_dve, 6)
            dve.tensor_scalar(moments[:, 2, :], moments[:, 2, :], 1.0 / F, EPS, ALU.mult, ALU.add).then_inc(s_std, 1)
            dve.wait_ge(s_std, 2)
            dve.reciprocal(moments[:, 2, :], moments[:, 2, :]).then_inc(s_dve, 1)
            dve.wait_ge(s_dve, 7)
            dve.scalar_tensor_tensor(out=moments[:, 3, :], in0=moments[:, 0, :], scalar=-0.5,
                                     in1=moments[:, 2, :], op0=ALU.mult, op1=ALU.mult).then_inc(s_rstd, 1)

            def copy_hT(c, b):
                dve.wait_ge(s_tr, chunk(c))
                dve.wait_ge(s_l1, chunk(c, 1))
                dve.tensor_copy(hT[:, :], tr_ps[:, 0:CHC]).then_inc(s_hT, 1)
                dve.wait_ge(s_h, chunk(c))
                xc = xs[:, bass.ds(c * CH, CH), :]
                dve.tensor_tensor(xc, xc, hs[:, b, :, :], ALU.add).then_inc(s_hx, 1)

            def add_bias(c):
                dve.wait_ge(s_l2, chunk(c))
                dve.wait_ge(s_tab, chunk(c, 1) * 16)
                dve.tensor_tensor(res[:, 0, :, :], l2_ps[:, 0:CHC].rearrange("p (t f) -> p t f", f=F),
                                  rows[:, 1:2, :].to_broadcast([P, CH, F]), ALU.add).then_inc(s_res, 1)

            dve.sem_inc(s_hT, 2)
            dve.sem_inc(s_hx, 2)
            dve.sem_inc(s_res, 2)
            dve.sem_inc(o_res, 2)
            dve.wait_ge(s_rows, 48)
            copy_hT(0, 0)
            with dve.Fori(0, (N_CHUNKS - 1) // 2) as pair:
                for k in range(2):
                    copy_hT(2 * pair + (k + 1), (k + 1) % 2)
                    add_bias(2 * pair + k)
            add_bias(N_CHUNKS - 1)

            dve.wait_ge(s_dst, 16)
            dve.tensor_copy(dst_f[:, :], dst_i[:, :]).then_inc(s_rel, 1)
            dve.wait_ge(s_base, 1)
            dve.tensor_tensor(rel[:, :].rearrange("p (g j) -> p g j", j=TPG),
                              dst_f[:, :].rearrange("p (g j) -> p g j", j=TPG),
                              misc_ps[:, 0:GROUPS].rearrange("p (g o) -> p g o", o=1).to_broadcast([P, GROUPS, TPG]),
                              ALU.subtract).then_inc(s_rel, 1)
            dve.wait_ge(s_rel, 2)
            dve.wait_ge(s_const, 5)

            dve.wait_ge(s_hx, chunk(N_CHUNKS - 1))
            with dve.Fori(0, N_CHUNKS) as c:
                xc = xs[:, bass.ds(c * CH, CH), :]
                dve.tensor_tensor(xc, xc, rows[:, 2:3, :].to_broadcast([P, CH, F]), ALU.add).then_inc(s_dve, 1)

            dve.sem_inc(msg_done, SLOTS)
            dve.sem_inc(win_added, SLOTS)

            def add_window(turn, s):
                dve.wait_ge(win_done, done(turn, s))
                dve.wait_ge(win_added, done(turn, s, 1))
                g = turn * SLOTS + s
                base = dve.value_load(dst_i[0:1, bass.ds(g * TPG, 1)], min_val=0, max_val=N_NODES)
                window = agg[:, bass.ds(base, WIN)]
                dve.tensor_tensor(window, window, sum_ps[ring_w[s]][:, 0:WIN], ALU.add).then_inc(win_added, 1)

            with dve.Fori(0, TURNS) as turn:
                for s in range(SLOTS):
                    b = ring_h[s]
                    dve.wait_ge(win_done, done(turn, s, back(ring_h, s)))
                    r = rel[:, bass.ds((turn * SLOTS + s) * TPG, TPG)].rearrange("p (j o) -> p j o", o=1)
                    dve.tensor_tensor(onehot[:, b, :, :],
                                      iota[:, 0:WIN].rearrange("p (o k) -> p o k", o=1).to_broadcast([P, TPG, WIN]),
                                      r.to_broadcast([P, TPG, WIN]), ALU.is_equal)
                    dve.wait_ge(gathered[s], turn * (16 * TPG) + 16 * TPG)
                    dve.wait_ge(fil_done, done(turn, s))
                    dve.tensor_tensor(msg[:, b, :], fil_ps[b], xg[:, s, :], ALU.mult).then_inc(msg_done, 1)
                    if s > 0:
                        add_window(turn, s - 1)
                add_window(turn, SLOTS - 1)

            dve.tensor_scalar(cover[:, :], rel[:, :], 0.0, None, ALU.is_ge).then_inc(s_cnt, 1)
            dve.wait_ge(s_cnt, 1)
            dve.scalar_tensor_tensor(out=cover[:, :], in0=rel[:, :], scalar=float(WIN), in1=cover[:, :],
                                     op0=ALU.is_lt, op1=ALU.mult).then_inc(s_cnt, 1)
            dve.wait_ge(s_cnt, 2)
            dve.reduce_sum(n_cover[:, :], cover[:, :], AX.X).then_inc(s_cnt, 1)
            dve.wait_ge(s_cnt, 4)
            dve.tensor_scalar(n_left[:, :], misc_ps[:, 1023:1024], -1.0, float(EDGE_TILES * P), ALU.mult,
                              ALU.add).then_inc(s_left, 1)
            dve.wait_ge(s_left, 1)
            n = dve.value_load(n_left[0:1, 0:1], min_val=0, max_val=EDGE_TILES * P)
            with dve.If(n > 0):
                dve.tensor_scalar(cover[:, :], cover[:, :], float(-2 * AGG), None, ALU.mult).then_inc(s_cnt, 1)
                dve.wait_ge(s_cnt, 5)
                dve.tensor_tensor(cover[:, :], cover[:, :], dst_f[:, :], ALU.add).then_inc(s_cnt, 1)
                dve.wait_ge(s_cnt, 6)
                dve.sem_inc(r_msg, 1)
                dve.sem_inc(r_win, 1)
                with dve.Fori(0, EDGE_TILES) as t:
                    dve.wait_ge(r_gat, t * 16 + 16)
                    dve.wait_ge(r_fil, t + 1)
                    dve.wait_ge(r_win, t * R_WINDOWS + 1)
                    dve.tensor_tensor(msg[:, 0, 0:P], fil_ps[0][:, 0:P], xg[:, 0, 0:P], ALU.mult).then_inc(r_msg, 1)
                    for k in range(R_WINDOWS):
                        dve.wait_ge(r_win, t * R_WINDOWS + (k + 1))
                        dve.tensor_scalar(r_oh[:, :], iota[:, :], float(k * RW), cover[:, bass.ds(t, 1)],
                                          ALU.add, ALU.is_equal).then_inc(r_one, 1)
                        dve.wait_ge(r_win, t * R_WINDOWS + (k + 2))
                        dve.tensor_tensor(agg[:, k * RW:(k + 1) * RW], agg[:, k * RW:(k + 1) * RW], sum_ps[0],
                                          ALU.add).then_inc(r_add, 1)
                        dve.wait_ge(r_add, t * R_WINDOWS + (k + 1))
            dve.wait_ge(win_added, done(TURNS - 1, SLOTS - 1))
            dve.sem_inc(s_agg, 1)

            dve.wait_ge(s_dve, 7 + N_CHUNKS)
            with dve.Fori(0, N_CHUNKS) as c:
                dve.wait_ge(o_l2, chunk(c))
                dve.wait_ge(o_out, chunk(c, 1) * 16)
                dve.tensor_tensor(res[:, 0, :, :], l2_ps[:, 0:CHC].rearrange("p (t f) -> p t f", f=F),
                                  xs[:, bass.ds(c * CH, CH), :], ALU.add).then_inc(o_res, 1)

        @block.tensor
        def _(pe):
            halves = ((0, 4 * P), (4 * P, CHC))

            def transposes(c, b):
                pe.wait_ge(s_h, chunk(c))
                pe.wait_ge(s_hT, chunk(c, 1))
                for j in range(CH):
                    i = pe.transpose(tr_ps[:, j * P:(j + 1) * P], hs[:, b, j, :], ident[:, :])
                i.then_inc(s_tr, 1)

            def layer1(src, weights, sem_out):
                for a, b in halves:
                    i = pe.matmul(l1_ps[:, a:b], weights, src(a, b), start=True, stop=True)
                i.then_inc(sem_out, 1)

            def layer2(weights, sem_out):
                for j in range(CH):
                    i = pe.matmul(l2_ps[:, j * P:(j + 1) * P], mid[:, j * P:(j + 1) * P], weights,
                                  start=True, stop=True)
                i.then_inc(sem_out, 1)

            def node_layer1(c):
                pe.wait_ge(s_hT, chunk(c))
                pe.wait_ge(s_mid, chunk(c, 1))
                layer1(lambda a, b: hT[:, a:b], w["aw1_s"][:, :], s_l1)

            def node_layer2(c):
                pe.wait_ge(s_mid, chunk(c))
                pe.wait_ge(s_res, chunk(c, 1))
                layer2(w["aw2_s"][:, :], s_l2)

            for used in (s_tr, s_l1, s_l2, o_l1, o_l2):
                pe.sem_inc(used, 2)
            pe.wait_ge(s_const, 3)
            pe.wait_ge(s_wts, 96)
            transposes(0, 0)
            with pe.Fori(0, (N_CHUNKS - 1) // 2) as pair:
                for k in range(2):
                    node_layer1(2 * pair + k)
                    transposes(2 * pair + (k + 1), (k + 1) % 2)
                    node_layer2(2 * pair + k)
            node_layer1(N_CHUNKS - 1)
            node_layer2(N_CHUNKS - 1)
            pe.wait_ge(s_rel, 1)
            pe.matmul(misc_ps[:, 0:GROUPS], ones[0:1, :],
                      dst_f[0:1, :].rearrange("p (g j) -> p g j", j=TPG)[:, :, 0], start=True, stop=True)\
                .then_inc(s_base, 1)

            pe.wait_ge(s_res, chunk(N_CHUNKS - 1))
            pe.wait_ge(s_rel, 2)
            pe.wait_ge(s_fb2, 3 * TPG)
            pe.sem_inc(hid_sum, SLOTS)
            pe.sem_inc(fil_done, SLOTS)
            pe.sem_inc(win_done, SLOTS)

            def hidden(turn, s):
                b = ring_h[s]
                if s in (0, SLOTS_A):
                    pe.wait_ge(attr_in[s // SLOTS_A], turn * 16 + 16)
                pe.wait_ge(hid_done, done(turn, s, back(ring_h, s)))
                pe.matmul(hid_ps[b], w["fw1_s"][:, :], attr[:, s * GC:(s + 1) * GC], start=True, stop=True)\
                    .then_inc(hid_sum, 1)

            def filters(turn, s):
                b = ring_h[s]
                pe.wait_ge(msg_done, done(turn, s, back(ring_h, s)))
                pe.wait_ge(hid_done, done(turn, s))
                for j in range(TPG):
                    pe.matmul(fil_ps[b][:, j * P:(j + 1) * P], hid[:, b, j * P:(j + 1) * P], w["fw2_s"][:, :],
                              start=(j == 0), stop=False)
                i = pe.matmul(fil_ps[b], ones_b[:, :], fb2_rows[:, :, :].rearrange("p j f -> p (j f)"), start=False,
                              stop=True)
                i.then_inc(fil_done, 1)

            def window(turn, s):
                b, k = ring_h[s], ring_w[s]
                pe.wait_ge(win_added, done(turn, s, back(ring_w, s)))
                pe.wait_ge(msg_done, done(turn, s))
                for j in range(TPG):
                    i = pe.matmul(sum_ps[k][:, 0:WIN], msg[:, b, j * P:(j + 1) * P], onehot[:, b, j, :],
                                  start=(j == 0), stop=(j == TPG - 1))
                i.then_inc(win_done, 1)

            with pe.Fori(0, TURNS) as turn:
                hidden(turn, 0)
                for s in range(SLOTS):
                    if s + 1 < SLOTS:
                        hidden(turn, s + 1)
                    filters(turn, s)
                    if s > 0:
                        window(turn, s - 1)
                window(turn, SLOTS - 1)

            pe.wait_ge(s_cnt, 3)
            pe.matmul(misc_ps[:, 1023:1024], ones[:, :], n_cover[:, :], start=True, stop=True).then_inc(s_cnt, 1)
            pe.wait_ge(s_left, 1)
            n = pe.value_load(n_left[0:1, 0:1], min_val=0, max_val=EDGE_TILES * P)
            with pe.If(n > 0):
                with pe.Fori(0, EDGE_TILES) as t:
                    pe.wait_ge(r_in, t * 32 + 32)
                    pe.matmul(hid_ps[0][:, 0:P], w["fw1_s"][:, :], attr[:, 0:P], start=True, stop=True)\
                        .then_inc(r_l1, 1)
                    pe.matmul(fil_ps[0][:, 0:P], ones_b[:, :], fb2_rows[:, 0, :], start=True, stop=False)
                    pe.wait_ge(r_hid, t + 1)
                    pe.matmul(fil_ps[0][:, 0:P], hid[:, 0, 0:P], w["fw2_s"][:, :], start=False, stop=True)\
                        .then_inc(r_fil, 1)
                    for k in range(R_WINDOWS):
                        pe.wait_ge(r_one, t * R_WINDOWS + (k + 1))
                        pe.matmul(sum_ps[0], msg[:, 0, 0:P], r_oh[:, :], start=True, stop=True).then_inc(r_win, 1)

            pe.wait_ge(s_agg, 1)
            def out_layer1(c):
                pe.wait_ge(o_mid, chunk(c, 1))
                layer1(lambda a, b: agg[:, bass.ds(c * CHC + a, b - a)], w["ow1_s"][:, :], o_l1)

            def out_layer2(c):
                pe.wait_ge(o_mid, chunk(c))
                pe.wait_ge(o_res, chunk(c, 1))
                layer2(w["ow2_s"][:, :], o_l2)

            out_layer1(0)
            with pe.Fori(0, N_CHUNKS - 1) as c:
                out_layer1(c + 1)
                out_layer2(c)
            out_layer2(N_CHUNKS - 1)


_W = ["fw1", "fb1", "fw2", "fb2", "aw1", "ab1", "aw2", "ab2", "ow1", "ob1", "ow2", "ob2"]


def kernel(x, src, dst, edge_attr_50, **weights):
    import concourse.bacc as bacc
    from concourse.bass_utils import run_bass_kernel_spmd

    pad = EDGE_TILES * P - N_EDGES
    src_p = np.concatenate([np.asarray(src), np.zeros(pad, np.asarray(src).dtype)])
    dst_p = np.concatenate([np.asarray(dst), np.full(pad, N_NODES, np.asarray(dst).dtype)])
    attr = np.zeros((NG, EDGE_TILES * P), np.asarray(edge_attr_50).dtype)
    attr[:, :N_EDGES] = np.asarray(edge_attr_50).T
    xp = np.zeros((NODE_TILES * P, F), np.asarray(x).dtype)
    xp[:N_NODES] = np.asarray(x)
    arrays = {
        "x": xp,
        "src": np.ascontiguousarray(src_p.reshape(TURNS, SLOTS * TPG, P).transpose(0, 2, 1)),
        "dst": np.ascontiguousarray(dst_p.reshape(EDGE_TILES, P).T),
        "attr": attr,
    }
    for n in _W:
        arrays[n] = np.ascontiguousarray(np.asarray(weights["L0_gnn_" + n]))

    nc = bacc.Bacc("TRN2", target_bir_lowering=False, num_devices=1)
    args = [nc.dram_tensor("in_" + n, a.shape, mybir.dt.from_np(a.dtype), kind="ExternalInput").ap()
            for n, a in arrays.items()]
    out = nc.dram_tensor("out", (NODE_TILES * P, F), mybir.dt.float32, kind="ExternalOutput").ap()
    gnn_layer(nc, *args, out)
    r = run_bass_kernel_spmd(nc, [{"in_" + n: a for n, a in arrays.items()}], core_ids=[0])
    return r.results[0]["out"][:N_NODES]
```

```python
import numpy as np
import concourse.bass as bass
from concourse import mybir
from contextlib import ExitStack

P = 128
F = 128
NG = 50
N_NODES = 6250
N_EDGES = 206250
NODE_TILES = -(-N_NODES // P)
CH = 7
N_CHUNKS = NODE_TILES // CH
CHC = CH * P
TPG = 4
GC = TPG * P
EDGE_TILES = -(-N_EDGES // GC) * TPG
GROUPS = EDGE_TILES // TPG
SLOTS = 13
TT = SLOTS * TPG
TURNS = GROUPS // SLOTS - 1
EARLY = TURNS * TT
SLOTS_A = 7
PARTS = ((0, SLOTS_A), (SLOTS_A, SLOTS))
WIN = 64
RW = 512
R_WINDOWS = -(-(N_NODES + 1) // RW)
AGG = max(R_WINDOWS * RW, N_NODES + WIN)
EPS = 1e-5
assert NODE_TILES == N_CHUNKS * CH and GROUPS == (TURNS + 1) * SLOTS

LEGS, LEG_TURNS, LEG_EARLY = 5, 5, 2
LEG_GROUPS = LEG_TURNS * SLOTS + LEG_EARLY
REST_TURNS = 3
REST_EARLY = SLOTS - LEGS * LEG_EARLY
LAST_TURNS = TURNS - LEGS * LEG_TURNS - REST_TURNS
assert LEGS == N_CHUNKS - 2 and LAST_TURNS > 0
CHECKPOINTS = [(c + 1) * LEG_TURNS * TT for c in range(LEGS)] + [(LEGS * LEG_TURNS + REST_TURNS) * TT]


def main_part(eng, turn, early, output, before_last):
    with eng.Fori(0, LEGS) as leg:
        with eng.Fori(0, LEG_TURNS) as t:
            turn(leg * LEG_GROUPS + t * SLOTS, leg * LEG_TURNS + t)
        mlp = leg * (LEG_EARLY + 1) + N_CHUNKS
        for r in range(LEG_EARLY):
            early(leg * LEG_GROUPS + (LEG_TURNS * SLOTS + r), leg * LEG_EARLY + r, r, mlp + r)
        output(leg * LEG_GROUPS + LEG_GROUPS, leg, mlp + LEG_EARLY)
    at, mlp = LEGS * LEG_GROUPS, N_CHUNKS + LEGS * (LEG_EARLY + 1)
    with eng.Fori(0, REST_TURNS) as t:
        turn(t * SLOTS + at, t + LEGS * LEG_TURNS)
    at += REST_TURNS * SLOTS
    for r in range(REST_EARLY):
        early(at + r, LEGS * LEG_EARLY + r, r, mlp + r)
    at += REST_EARLY
    output(at, LEGS, mlp + REST_EARLY)
    before_last()
    with eng.Fori(0, LAST_TURNS) as t:
        turn(t * SLOTS + at, t + (TURNS - LAST_TURNS))


LAST_MLP = N_CHUNKS + LEGS * (LEG_EARLY + 1) + REST_EARLY + 1

RING3 = [s % 2 for s in range(SLOTS - 1)] + [2]
RING2 = [s % 2 for s in range(SLOTS)]


def back(ring, s):
    return next(d for d in range(1, SLOTS + 1) if ring[(s - d) % SLOTS] == ring[s])


def done(place, s=0, d=0):
    return place + (SLOTS + 1 + s - d)


def run(c, d=0):
    return c + (3 - d)


def gnn_layer(nc, x, src_t, dst_t, attr_t, fw1, fb1, fw2, fb2, aw1, ab1, aw2, ab2, ow1, ob1, ow2, ob2, out):
    f32, i32, bf16 = mybir.dt.float32, mybir.dt.int32, mybir.dt.bfloat16
    ALU, ACT, AX = mybir.AluOpType, mybir.ActivationFunctionType, mybir.AxisListType

    table = nc.dram_tensor("node_table", [NODE_TILES * P, F], f32).ap()
    x_tiles = x.rearrange("(t p) f -> p t f", p=P)
    out_tiles = out.rearrange("(t p) f -> p t f", p=P)
    table_tiles = table.rearrange("(t p) f -> p t f", p=P)

    with ExitStack() as ctx:
        def sb(name, shape, dt=f32):
            return ctx.enter_context(nc.sbuf_tensor(name, shape, dt))

        def sem(name):
            return ctx.enter_context(nc.semaphore(name))

        ident = sb("ident", [P, P])
        ones = sb("ones", [P, P])
        ones_b = sb("ones_b", [P, P], bf16)
        iota = sb("iota", [P, RW])
        w = {n: sb(n, [a.shape[0], F]) for n, a in
             (("fw1_s", fw1), ("fw2_s", fw2), ("aw1_s", aw1), ("aw2_s", aw2), ("ow1_s", ow1), ("ow2_s", ow2))}
        cols = sb("cols", [P, 3])
        rows = sb("rows", [P, 3, F])
        fb2_part = sb("fb2_part", [P, 3, F], bf16)
        fb2_rest = sb("fb2_rest", [P, 2, F])
        fb2_rows = sb("fb2_rows", [P, TPG, F], bf16)
        xs = sb("xs", [P, NODE_TILES, F])
        hs = sb("hs", [P, 2, CH, F])
        hT = sb("hT", [P, CHC])
        mid = sb("mid", [P, CHC])
        res = sb("res", [P, CH, F])
        stats = sb("stats", [P, TT, 6])
        moments = sb("moments", [P, 4, NODE_TILES])
        dst_i = sb("dst_i", [P, EDGE_TILES], i32)
        first_dst = sb("first_dst", [1, GROUPS])
        rel = sb("rel", [P, EDGE_TILES])
        cover = sb("cover", [P, EDGE_TILES], bf16)
        in_order = sb("in_order", [P, EDGE_TILES], bf16)
        n_well = sb("n_well", [P, 1])
        n_left = sb("n_left", [P, 1], i32)
        agg = sb("agg", [P, AGG])
        src_ab = [sb("src_a", [P, SLOTS_A * TPG], i32), sb("src_b", [P, (SLOTS - SLOTS_A) * TPG], i32)]
        attr = sb("attr", [NG, SLOTS * GC])
        xg = sb("xg", [P, SLOTS, GC])
        hid = sb("hid", [P, 3, GC])
        msg = sb("msg", [P, 3, GC])
        onehot = sb("onehot", [P, 3, TPG, WIN])
        e_src = sb("e_src", [P, TT], i32)
        e_x = sb("e_x", [P, TT, F])
        e_moments = sb("e_moments", [P, 4, TT])
        e_attr = sb("e_attr", [NG, 2, GC])
        e_row = sb("e_row", [P, GC])
        r_src = src_ab[0][:, 0:1]
        r_onehot = msg[:, 1, :]
        r_dst = xg[:, 1:5, :].rearrange("p s c -> p (s c)")[:, 0:EDGE_TILES]

        banks = [ctx.enter_context(nc.psum_tensor(f"banks{i}", [P, 1024], f32)) for i in range(4)]
        bank = [banks[i // 2][:, 512 * (i % 2):512 * (i % 2) + 512] for i in range(8)]
        hid_ps, fil_ps, sum_ps = bank[0:3], bank[3:6], bank[6:8]
        l1_ps, tr_ps, l2_ps, misc_ps = banks
        e_l1_ps, e_tr_ps, e_l2_ps = bank[0], bank[3], bank[4]

        s_wts, s_cols, s_rows, s_dst = sem("s_wts"), sem("s_cols"), sem("s_rows"), sem("s_dst")
        s_x = [sem(f"s_x{i}") for i in range(N_CHUNKS)]
        s_pool, s_set, s_base, s_rel, s_cover, s_left = (
            sem(n) for n in ("s_pool", "s_set", "s_base", "s_rel", "s_cover", "s_left"))
        s_fb2, s_res_in, s_var, s_std, s_rstd = (sem(n) for n in ("s_fb2", "s_res_in", "s_var", "s_std", "s_rstd"))
        s_h, s_hx, s_tr, s_hT, s_l1, s_mid, s_l2, s_res = (
            sem(n) for n in ("s_h", "s_hx", "s_tr", "s_hT", "s_l1", "s_mid", "s_l2", "s_res"))
        s_tab, s_out = sem("s_tab"), sem("s_out")
        attr_in, src_in = [sem("attr_in_a"), sem("attr_in_b")], [sem("src_in_a"), sem("src_in_b")]
        gathered = [sem(f"gathered{s}") for s in range(SLOTS)]
        slot_taken, hid_sum, hid_done, fil_done, msg_done, win_done, win_added = (
            sem(n) for n in ("slot_taken", "hid_sum", "hid_done", "fil_done", "msg_done", "win_done", "win_added"))
        e_src_in = sem("e_src_in")
        e_attr_in = [sem("e_attr_in0"), sem("e_attr_in1")]
        r_key, r_in, r_gat, r_l1, r_hid, r_fil, r_msg, r_one, r_win, r_add = (
            sem(n) for n in ("r_key", "r_in", "r_gat", "r_l1", "r_hid", "r_fil", "r_msg", "r_one", "r_win", "r_add"))
        a_l1, a_mid, a_l2, a_res, a_out = (sem(n) for n in ("a_l1", "a_mid", "a_l2", "a_res", "a_out"))

        def edges_left(eng):
            eng.wait_ge(s_left, 1)
            return eng.value_load(n_left[0:1, 0:1], min_val=0, max_val=EDGE_TILES * P)

        block = ctx.enter_context(nc.Block())

        @block.sync
        def _(sp):
            sp.dma_start(e_src[:, :], src_t[TURNS, :, :]).then_inc(e_src_in, 16)
            for c in range(N_CHUNKS):
                sp.dma_start(xs[:, c * CH:(c + 1) * CH, :], x_tiles[:, c * CH:(c + 1) * CH, :]).then_inc(s_x[c], 16)
            sp.sem_inc(s_tab, 32)
            with sp.Fori(0, N_CHUNKS) as c:
                sp.wait_ge(s_res, run(c))
                sp.dma_start(table_tiles[:, bass.ds(c * CH, CH), :], res[:, :, :]).then_inc(s_tab, 16)

            def turn(place, n):
                for k, (a, b) in enumerate(PARTS):
                    for s in range(a, b):
                        sp.wait_ge(gathered[s], n * (16 * TPG) + 16 * TPG)
                    sp.dma_start(src_ab[k][:, :], src_t[bass.ds(n, 1), :, a * TPG:b * TPG]
                                 .rearrange("o p j -> p (o j)")).then_inc(src_in[k], 16)
                    sp.wait_ge(hid_sum, done(place, b - 1, SLOTS))
                    sp.dma_start(attr[:, a * GC:b * GC], attr_t[:, bass.ds(n * (SLOTS * GC) + a * GC, (b - a) * GC)])\
                        .then_inc(attr_in[k], 16)

            def early(place, n, r, mlp):
                sp.wait_ge(hid_sum, done(place, 0, SLOTS if r < 2 else 2))
                sp.dma_start(e_attr[:, r % 2, :], attr_t[:, bass.ds(n * GC + EARLY * P, GC)]).then_inc(e_attr_in[r % 2], 16)

            main_part(sp, turn, early, lambda *_: None, lambda: None)
            n = edges_left(sp)
            with sp.If(n > 0):
                with sp.Fori(0, TURNS + 1) as turn:
                    with sp.Fori(0, TT) as j:
                        t = turn * TT + j
                        sp.wait_ge(r_msg, t + 1)
                        sp.dma_start(r_src, src_t[bass.ds(turn, 1), :, bass.ds(j, 1)].rearrange("o p j -> p (o j)"),
                                     allow_slow_non_contiguous=True).then_inc(r_in, 16)
                        sp.dma_start(attr[:, 0:P], attr_t[:, bass.ds(t * P, P)]).then_inc(r_in, 16)

        @block.gpsimd
        def _(pool):
            pool.memset(ident[:, :], 0.0).then_inc(s_pool, 1)
            pool.iota(iota[:, :], pattern=[[1, RW]], base=0, channel_multiplier=0,
                      allow_small_or_imprecise_dtypes=True).then_inc(s_pool, 1)
            pool.wait_ge(s_pool, 2)
            pool.affine_select(out=ident[:, :], in_=ident[:, :], compare_op=ALU.not_equal, fill=1.0, base=0,
                               pattern=[[-1, P]], channel_multiplier=1).then_inc(s_pool, 1)
            pool.wait_ge(s_pool, 3)
            pool.wait_ge(e_src_in, 16)
            for j in range(TT):
                pool.indirect_dma_start(e_x[:, j, :], None, x[:, :],
                                        bass.IndirectOffsetOnAxis(ap=e_src[:, j:j + 1], axis=0)).then_inc(gathered[j // TPG], 16)
            pool.wait_ge(s_tab, 16 * run(N_CHUNKS - 1))

            def turn(place, n):
                for s in range(SLOTS):
                    k = s // SLOTS_A
                    if s in (0, SLOTS_A):
                        pool.wait_ge(src_in[k], n * 16 + 16)
                    pool.wait_ge(msg_done, done(place, s, SLOTS))
                    pool.sem_inc(slot_taken, 1)
                    for j in range(TPG):
                        col = (s - k * SLOTS_A) * TPG + j
                        pool.indirect_dma_start(xg[:, s, j * P:(j + 1) * P], None, table[:, :],
                                                bass.IndirectOffsetOnAxis(ap=src_ab[k][:, col:col + 1], axis=0))\
                            .then_inc(gathered[s], 16)

            main_part(pool, turn, lambda *_: None, lambda *_: None, lambda: None)
            n = edges_left(pool)
            with pool.If(n > 0):
                with pool.Fori(0, EDGE_TILES) as t:
                    pool.wait_ge(r_in, t * 32 + 32)
                    pool.wait_ge(r_msg, t + 1)
                    pool.sem_inc(slot_taken, 1)
                    pool.indirect_dma_start(xg[:, 0, 0:P], None, table[:, :],
                                            bass.IndirectOffsetOnAxis(ap=r_src, axis=0)).then_inc(r_gat, 16)

        @block.scalar
        def _(act):
            for name, a in (("aw1_s", aw1), ("aw2_s", aw2)):
                act.dma_start(w[name][:, :], a).then_inc(s_wts, 16)
            for i, b in enumerate((fb2, ab2, ob2)):
                act.dma_start(rows[:, i, :], b.rearrange("(o f) -> o f", o=1).to_broadcast([P, F])).then_inc(s_rows, 16)
            for i, b in enumerate((fb1, ab1, ob1)):
                act.dma_start(cols[:, i:i + 1], b.rearrange("(f o) -> f o", o=1)).then_inc(s_cols, 16)
            act.dma_start(dst_i[:, :], dst_t).then_inc(s_dst, 16)
            for name, a in (("fw1_s", fw1), ("fw2_s", fw2), ("ow1_s", ow1), ("ow2_s", ow2)):
                act.dma_start(w[name][:, :], a).then_inc(s_wts, 16)
            for ahead in (s_h, s_mid, a_mid):
                act.sem_inc(ahead, 2)
            act.sem_inc(s_out, 32)
            act.sem_inc(a_out, 32)
            act.sem_inc(hid_done, SLOTS)
            act.wait_ge(s_var, 1)
            act.activation(moments[:, 2, :], moments[:, 2, :], ACT.Sqrt).then_inc(s_std, 1)

            def relu_ln(c, b):
                act.wait_ge(s_tr, run(c, 2))
                act.wait_ge(s_hx, run(c, 2))
                for j in range(CH):
                    t = c * CH + j
                    i = act.activation(hs[:, b, j, :], xs[:, bass.ds(t, 1), :].rearrange("p o f -> p (o f)"), ACT.Relu,
                                       bias=moments[:, 3, bass.ds(t, 1)], scale=moments[:, 2, bass.ds(t, 1)])
                i.then_inc(s_h, 1)

            def silu_mid(mlp, n, bias, summed=s_l1, used=s_l2, mid_done=s_mid):
                act.wait_ge(summed, run(mlp))
                act.wait_ge(used, run(mlp, 1))
                act.activation(mid[:, 0:n], l1_ps[:, 0:n], ACT.Silu, bias=cols[:, bias:bias + 1]).then_inc(mid_done, 1)

            act.wait_ge(s_rstd, 1)
            act.wait_ge(s_cols, 48)
            relu_ln(0, 0)
            relu_ln(1, 1)
            with act.Fori(0, N_CHUNKS // 2 - 1) as pair:
                for k in range(2):
                    silu_mid(2 * pair + k, CHC, 1)
                    relu_ln(2 * pair + (k + 2), k)
            silu_mid(N_CHUNKS - 3, CHC, 1)
            relu_ln(N_CHUNKS - 1, 0)
            silu_mid(N_CHUNKS - 2, CHC, 1)
            silu_mid(N_CHUNKS - 1, CHC, 1)
            act.wait_ge(s_var, 2)
            act.activation(e_moments[:, 2, :], e_moments[:, 2, :], ACT.Sqrt).then_inc(s_std, 1)

            def silu_hid(place, s, b, d):
                act.wait_ge(hid_sum, done(place, s))
                act.wait_ge(fil_done, done(place, s, d))
                act.activation(hid[:, b, :], hid_ps[b], ACT.Silu, bias=cols[:, 0:1]).then_inc(hid_done, 1)

            def turn(place, n):
                for s in range(SLOTS):
                    silu_hid(place, s, RING3[s], back(RING3, s))

            def early(place, n, r, mlp):
                silu_hid(place, 0, 2, 1)
                act.wait_ge(s_rstd, 2)
                act.wait_ge(s_tr, run(n, 1) + N_CHUNKS)
                for j in range(TPG):
                    t = n * TPG + j
                    i = act.activation(hs[:, 0, j, :], e_x[:, bass.ds(t, 1), :].rearrange("p o f -> p (o f)"), ACT.Relu,
                                       bias=e_moments[:, 3, bass.ds(t, 1)], scale=e_moments[:, 2, bass.ds(t, 1)])
                i.then_inc(s_h, 1)
                silu_mid(mlp, GC, 1)

            def output(place, c, mlp):
                silu_mid(mlp, CHC, 2)
                act.wait_ge(s_res, run(mlp))
                act.dma_start(out_tiles[:, bass.ds(c * CH, CH), :], res[:, :, :]).then_inc(s_out, 16)

            act.wait_ge(s_hx, run(N_CHUNKS - 1))
            main_part(act, turn, early, output, lambda: None)
            n = edges_left(act)
            with act.If(n > 0):
                with act.Fori(0, EDGE_TILES) as t:
                    act.wait_ge(r_l1, t + 1)
                    act.activation(hid[:, 0, 0:P], hid_ps[0][:, 0:P], ACT.Silu, bias=cols[:, 0:1]).then_inc(r_hid, 1)
                act.wait_ge(s_out, 16 * run(N_CHUNKS - 2))
                with act.Fori(0, N_CHUNKS - 1) as c:
                    silu_mid(c, CHC, 2, a_l1, a_l2, a_mid)
                    act.wait_ge(a_res, run(c))
                    act.dma_start(out_tiles[:, bass.ds(c * CH, CH), :], res[:, :, :]).then_inc(a_out, 16)
                act.wait_ge(a_out, 16 * run(N_CHUNKS - 2))
            output(GROUPS, N_CHUNKS - 1, LAST_MLP)
            act.wait_ge(s_out, 16 * run(N_CHUNKS - 1))

        @block.vector
        def _(dve):
            dve.memset(ones[:, :], 1.0)
            dve.memset(ones_b[:, :], 1.0)
            dve.memset(fb2_rows[:, :, :], 0.0)
            dve.memset(in_order[:, 0:CHECKPOINTS[0]], 0.0)
            for c, (a, b) in enumerate(zip(CHECKPOINTS, CHECKPOINTS[1:] + [EDGE_TILES])):
                dve.memset(in_order[:, a:b], float((c + 1) * CHC))
            dve.memset(agg[:, :], 0.0).then_inc(s_set, 1)
            for ahead in (s_hT, s_hx, s_res, a_res):
                dve.sem_inc(ahead, 2)
            dve.sem_inc(msg_done, SLOTS)
            dve.sem_inc(win_added, SLOTS)

            step = [0]

            def moments_of(st, m):
                def link(i):
                    step[0] += 1
                    i.then_inc(s_res_in, 1)
                    dve.wait_ge(s_res_in, step[0])

                link(dve.tensor_tensor(m[:, 0, :], st[:, :, 1], st[:, :, 4], ALU.add))
                link(dve.tensor_tensor(m[:, 1, :], st[:, :, 1], st[:, :, 4], ALU.subtract))
                link(dve.tensor_tensor(m[:, 2, :], st[:, :, 2], st[:, :, 5], ALU.add))
                link(dve.tensor_tensor(m[:, 1, :], m[:, 1, :], m[:, 1, :], ALU.mult))
                link(dve.scalar_tensor_tensor(out=m[:, 2, :], in0=m[:, 1, :], scalar=F / 4.0, in1=m[:, 2, :],
                                              op0=ALU.mult, op1=ALU.add))
                dve.tensor_scalar(m[:, 2, :], m[:, 2, :], 1.0 / F, EPS, ALU.mult, ALU.add).then_inc(s_var, 1)

            def scales_of(m, n_std):
                dve.wait_ge(s_std, n_std)
                dve.reciprocal(m[:, 2, :], m[:, 2, :]).then_inc(s_res_in, 1)
                step[0] += 1
                dve.wait_ge(s_res_in, step[0])
                dve.scalar_tensor_tensor(out=m[:, 3, :], in0=m[:, 0, :], scalar=-0.5, in1=m[:, 2, :],
                                         op0=ALU.mult, op1=ALU.mult).then_inc(s_rstd, 1)

            for c in range(N_CHUNKS):
                dve.wait_ge(s_x[c], 16)
                for t in range(c * CH, (c + 1) * CH):
                    i = dve.bn_stats(stats[:, t, :], xs[:, t, :])
            i.then_inc(s_res_in, 1)
            step[0] += 1
            dve.wait_ge(s_res_in, step[0])
            moments_of(stats[:, 0:NODE_TILES, :], moments)
            scales_of(moments, 1)

            def copy_hT(c, b):
                dve.wait_ge(s_tr, run(c))
                dve.wait_ge(s_l1, run(c, 1))
                dve.tensor_copy(hT[:, :], tr_ps[:, 0:CHC]).then_inc(s_hT, 1)
                dve.wait_ge(s_h, run(c))
                xc = xs[:, bass.ds(c * CH, CH), :]
                dve.tensor_tensor(xc, xc, hs[:, b, :, :], ALU.add).then_inc(s_hx, 1)

            def add_bias(c):
                dve.wait_ge(s_l2, run(c))
                dve.wait_ge(s_tab, run(c, 1) * 16)
                dve.tensor_tensor(res[:, :, :], l2_ps[:, 0:CHC].rearrange("p (t f) -> p t f", f=F),
                                  rows[:, 1:2, :].to_broadcast([P, CH, F]), ALU.add).then_inc(s_res, 1)

            dve.wait_ge(s_rows, 48)
            copy_hT(0, 0)
            with dve.Fori(0, (N_CHUNKS - 1) // 2) as pair:
                for k in range(2):
                    copy_hT(2 * pair + (k + 1), (k + 1) % 2)
                    add_bias(2 * pair + k)
            add_bias(N_CHUNKS - 1)

            dve.wait_ge(s_dst, 16)
            dve.tensor_copy(first_dst[:, :], dst_i[0:1, :].rearrange("p (g j) -> p g j", j=TPG)[:, :, 0]).then_inc(s_rel, 1)
            dve.tensor_copy(fb2_part[:, 0, :], rows[:, 0, :]).then_inc(s_fb2, 1)
            dve.wait_ge(s_fb2, 1)
            dve.tensor_tensor(fb2_rest[:, 0, :], rows[:, 0, :], fb2_part[:, 0, :], ALU.subtract).then_inc(s_fb2, 1)
            dve.wait_ge(s_fb2, 2)
            dve.tensor_copy(fb2_part[:, 1, :], fb2_rest[:, 0, :]).then_inc(s_fb2, 1)
            dve.wait_ge(s_fb2, 3)
            dve.tensor_tensor(fb2_rest[:, 1, :], fb2_rest[:, 0, :], fb2_part[:, 1, :], ALU.subtract).then_inc(s_fb2, 1)
            dve.wait_ge(s_fb2, 4)
            dve.tensor_copy(fb2_part[:, 2, :], fb2_rest[:, 1, :]).then_inc(s_fb2, 1)
            dve.wait_ge(s_fb2, 5)
            dve.wait_ge(s_set, 1)
            for i in range(3):
                dve.tensor_copy(fb2_rows[32 * i:32 * i + 1, :, :],
                                fb2_part[32 * i:32 * i + 1, i:i + 1, :].to_broadcast([1, TPG, F])).then_inc(s_fb2, 1)

            dve.wait_ge(s_base, 1)
            dve.tensor_tensor(rel[:, :].rearrange("p (g j) -> p g j", j=TPG),
                              dst_i[:, :].rearrange("p (g j) -> p g j", j=TPG),
                              misc_ps[:, 0:GROUPS].rearrange("p (g o) -> p g o", o=1).to_broadcast([P, GROUPS, TPG]),
                              ALU.subtract).then_inc(s_rel, 1)

            for t in range(TT):
                if t % TPG == 0:
                    dve.wait_ge(gathered[t // TPG], 16 * TPG)
                i = dve.bn_stats(stats[:, t, :], e_x[:, t, :])
            i.then_inc(s_res_in, 1)
            step[0] += 1
            dve.wait_ge(s_res_in, step[0])
            moments_of(stats, e_moments)
            scales_of(e_moments, 2)

            dve.wait_ge(s_rel, 2)
            dve.tensor_scalar(cover[:, :], rel[:, :], 0.0, None, ALU.is_ge).then_inc(s_cover, 1)
            dve.wait_ge(s_cover, 1)
            dve.scalar_tensor_tensor(out=cover[:, :], in0=rel[:, :], scalar=float(WIN), in1=cover[:, :],
                                     op0=ALU.is_lt, op1=ALU.mult).then_inc(s_cover, 1)
            dve.tensor_tensor(in_order[:, :], dst_i[:, :], in_order[:, :], ALU.is_ge).then_inc(s_cover, 1)
            dve.wait_ge(s_cover, 3)
            dve.tensor_tensor(in_order[:, :], in_order[:, :], cover[:, :], ALU.mult).then_inc(s_cover, 1)
            dve.wait_ge(s_cover, 4)
            dve.reduce_sum(n_well[:, :], in_order[:, :], AX.X).then_inc(s_cover, 1)

            dve.wait_ge(s_hx, run(N_CHUNKS - 1))
            for c in range(N_CHUNKS):
                xc = xs[:, c * CH:(c + 1) * CH, :]
                i = dve.tensor_tensor(xc, xc, rows[:, 2:3, :].to_broadcast([P, CH, F]), ALU.add)
            i.then_inc(s_res_in, 1)
            step[0] += 1
            dve.wait_ge(s_res_in, step[0])
            dve.wait_ge(s_cover, 6)
            dve.tensor_scalar(n_left[:, :], misc_ps[:, 1023:1024], -1.0, float(EDGE_TILES * P), ALU.mult,
                              ALU.add).then_inc(s_left, 1)
            dve.wait_ge(s_pool, 3)
            dve.wait_ge(s_tab, 16 * run(N_CHUNKS - 1))

            def one_hot(place, s, b, tile, d):
                dve.wait_ge(win_done, done(place, s, d))
                r = rel[:, bass.ds(tile, TPG)].rearrange("p (j o) -> p j o", o=1)
                dve.tensor_tensor(onehot[:, b, :, :],
                                  iota[:, 0:WIN].rearrange("p (o k) -> p o k", o=1).to_broadcast([P, TPG, WIN]),
                                  r.to_broadcast([P, TPG, WIN]), ALU.is_equal)

            def add_window(place, s, k, tile):
                dve.wait_ge(win_done, done(place, s))
                dve.wait_ge(win_added, done(place, s, 1))
                base = dve.value_load(dst_i[0:1, bass.ds(tile, 1)], min_val=0, max_val=N_NODES)
                window = agg[:, bass.ds(base, WIN)]
                dve.tensor_tensor(window, window, sum_ps[k][:, 0:WIN], ALU.add).then_inc(win_added, 1)

            def turn(place, n):
                for s in range(SLOTS):
                    b = RING3[s]
                    one_hot(place, s, b, n * TT + s * TPG, back(RING3, s))
                    dve.wait_ge(gathered[s], n * (16 * TPG) + 32 * TPG)
                    dve.wait_ge(fil_done, done(place, s))
                    dve.tensor_tensor(msg[:, b, :], fil_ps[b], xg[:, s, :], ALU.mult).then_inc(msg_done, 1)
                    if s > 0:
                        add_window(place, s - 1, RING2[s - 1], n * TT + (s - 1) * TPG)
                add_window(place, SLOTS - 1, RING2[SLOTS - 1], n * TT + (SLOTS - 1) * TPG)

            def early(place, n, r, mlp):
                dve.wait_ge(s_tr, run(n) + N_CHUNKS)
                dve.wait_ge(s_l1, run(mlp, 1))
                dve.tensor_copy(hT[:, 0:GC], e_tr_ps).then_inc(s_hT, 1)
                one_hot(place, 0, 2, n * TPG + EARLY, 1)
                dve.wait_ge(s_l2, run(mlp))
                dve.tensor_tensor(e_row[:, :].rearrange("p (j f) -> p j f", f=F),
                                  e_l2_ps.rearrange("p (j f) -> p j f", f=F),
                                  rows[:, 1:2, :].to_broadcast([P, TPG, F]), ALU.add).then_inc(s_res, 1)
                dve.wait_ge(s_res, run(mlp))
                dve.wait_ge(fil_done, done(place))
                dve.tensor_tensor(msg[:, 2, :], fil_ps[2], e_row[:, :], ALU.mult).then_inc(msg_done, 1)
                add_window(place, 0, 0, n * TPG + EARLY)

            def output(place, c, mlp):
                dve.wait_ge(s_l2, run(mlp))
                dve.wait_ge(s_out, run(c, 1) * 16)
                dve.tensor_tensor(res[:, :, :], l2_ps[:, 0:CHC].rearrange("p (t f) -> p t f", f=F),
                                  xs[:, bass.ds(c * CH, CH), :], ALU.add).then_inc(s_res, 1)

            main_part(dve, turn, early, output, lambda: None)
            n = edges_left(dve)
            with dve.If(n > 0):
                dve.wait_ge(msg_done, done(GROUPS - 1))
                dve.tensor_scalar(r_dst, cover[:, :], float(-2 * AGG), None, ALU.mult).then_inc(r_key, 1)
                dve.wait_ge(r_key, 1)
                dve.tensor_tensor(r_dst, r_dst, dst_i[:, :], ALU.add).then_inc(r_key, 1)
                dve.wait_ge(r_key, 2)
                dve.wait_ge(win_added, done(GROUPS - 1))
                dve.sem_inc(r_msg, 1)
                dve.sem_inc(r_win, 1)
                with dve.Fori(0, EDGE_TILES) as t:
                    dve.wait_ge(r_gat, t * 16 + 16)
                    dve.wait_ge(r_fil, t + 1)
                    dve.wait_ge(r_win, t * R_WINDOWS + 1)
                    dve.tensor_tensor(msg[:, 0, 0:P], fil_ps[0][:, 0:P], xg[:, 0, 0:P], ALU.mult).then_inc(r_msg, 1)
                    for k in range(R_WINDOWS):
                        dve.wait_ge(r_win, t * R_WINDOWS + (k + 1))
                        dve.tensor_scalar(r_onehot, iota[:, :], float(k * RW), r_dst[:, bass.ds(t, 1)],
                                          ALU.add, ALU.is_equal).then_inc(r_one, 1)
                        dve.wait_ge(r_win, t * R_WINDOWS + (k + 2))
                        dve.tensor_tensor(agg[:, k * RW:(k + 1) * RW], agg[:, k * RW:(k + 1) * RW], sum_ps[0],
                                          ALU.add).then_inc(r_add, 1)
                        dve.wait_ge(r_add, t * R_WINDOWS + (k + 1))
                dve.wait_ge(s_out, 16 * run(N_CHUNKS - 2))
                with dve.Fori(0, N_CHUNKS - 1) as c:
                    dve.wait_ge(a_l2, run(c))
                    dve.wait_ge(a_out, run(c, 1) * 16)
                    dve.tensor_tensor(res[:, :, :], l2_ps[:, 0:CHC].rearrange("p (t f) -> p t f", f=F),
                                      xs[:, bass.ds(c * CH, CH), :], ALU.add).then_inc(a_res, 1)
                dve.wait_ge(a_out, 16 * run(N_CHUNKS - 2))
            output(GROUPS, N_CHUNKS - 1, LAST_MLP)

        @block.tensor
        def _(pe):
            halves = ((0, 4 * P), (4 * P, CHC))

            def transposes(to, b, n_tiles):
                for j in range(n_tiles):
                    i = pe.transpose(to[:, j * P:(j + 1) * P], hs[:, b, j, :], ident[:, :])
                i.then_inc(s_tr, 1)

            def layer1(src, weights, summed):
                for a, b in halves:
                    i = pe.matmul(l1_ps[:, a:b], weights, src(a, b), start=True, stop=True)
                i.then_inc(summed, 1)

            def layer2(to, n_tiles, weights, summed):
                for j in range(n_tiles):
                    i = pe.matmul(to[:, j * P:(j + 1) * P], mid[:, j * P:(j + 1) * P], weights, start=True, stop=True)
                i.then_inc(summed, 1)

            def node_transposes(c, b):
                pe.wait_ge(s_h, run(c))
                pe.wait_ge(s_hT, run(c, 1))
                transposes(tr_ps, b, CH)

            def node_layer1(c):
                pe.wait_ge(s_hT, run(c))
                pe.wait_ge(s_mid, run(c, 1))
                layer1(lambda a, b: hT[:, a:b], w["aw1_s"][:, :], s_l1)

            def node_layer2(c):
                pe.wait_ge(s_mid, run(c))
                pe.wait_ge(s_res, run(c, 1))
                layer2(l2_ps, CH, w["aw2_s"][:, :], s_l2)

            for ahead in (s_tr, s_l1, s_l2, a_l1, a_l2):
                pe.sem_inc(ahead, 2)
            for ahead in (hid_sum, fil_done, win_done):
                pe.sem_inc(ahead, SLOTS)
            pe.wait_ge(s_pool, 3)
            pe.wait_ge(s_wts, 96)
            node_transposes(0, 0)
            with pe.Fori(0, (N_CHUNKS - 1) // 2) as pair:
                for k in range(2):
                    node_layer1(2 * pair + k)
                    node_transposes(2 * pair + (k + 1), (k + 1) % 2)
                    node_layer2(2 * pair + k)
            node_layer1(N_CHUNKS - 1)
            node_layer2(N_CHUNKS - 1)
            pe.wait_ge(s_set, 1)
            pe.wait_ge(s_rel, 1)
            pe.matmul(misc_ps[:, 0:GROUPS], ones[0:1, :], first_dst[:, :], start=True, stop=True).then_inc(s_base, 1)
            pe.wait_ge(s_cover, 5)
            pe.matmul(misc_ps[:, 1023:1024], ones[:, :], n_well[:, :], start=True, stop=True).then_inc(s_cover, 1)
            pe.wait_ge(s_left, 1)
            pe.wait_ge(s_res, run(N_CHUNKS - 1))
            pe.wait_ge(s_fb2, 8)

            def hidden(place, s, b, features, d):
                pe.wait_ge(hid_done, done(place, s, d))
                pe.matmul(hid_ps[b], w["fw1_s"][:, :], features, start=True, stop=True).then_inc(hid_sum, 1)

            def filters(place, s, b, d):
                pe.wait_ge(msg_done, done(place, s, d))
                pe.wait_ge(hid_done, done(place, s))
                for j in range(TPG):
                    pe.matmul(fil_ps[b][:, j * P:(j + 1) * P], hid[:, b, j * P:(j + 1) * P], w["fw2_s"][:, :],
                              start=(j == 0), stop=False)
                pe.matmul(fil_ps[b], ones_b[:, :], fb2_rows[:, :, :].rearrange("p j f -> p (j f)"), start=False,
                          stop=True).then_inc(fil_done, 1)

            def window(place, s, b, k, d):
                pe.wait_ge(win_added, done(place, s, d))
                pe.wait_ge(msg_done, done(place, s))
                for j in range(TPG):
                    i = pe.matmul(sum_ps[k][:, 0:WIN], msg[:, b, j * P:(j + 1) * P], onehot[:, b, j, :],
                                  start=(j == 0), stop=(j == TPG - 1))
                i.then_inc(win_done, 1)

            def turn_hidden(place, n, s):
                if s in (0, SLOTS_A):
                    pe.wait_ge(attr_in[s // SLOTS_A], n * 16 + 16)
                hidden(place, s, RING3[s], attr[:, s * GC:(s + 1) * GC], back(RING3, s))

            def turn(place, n):
                turn_hidden(place, n, 0)
                for s in range(SLOTS):
                    if s + 1 < SLOTS:
                        turn_hidden(place, n, s + 1)
                    filters(place, s, RING3[s], back(RING3, s))
                    if s > 0:
                        window(place, s - 1, RING3[s - 1], RING2[s - 1], back(RING2, s - 1))
                window(place, SLOTS - 1, RING3[SLOTS - 1], RING2[SLOTS - 1], back(RING2, SLOTS - 1))

            def early(place, n, r, mlp):
                pe.wait_ge(e_attr_in[r % 2], e_attr_loads(n, r))
                hidden(place, 0, 2, e_attr[:, r % 2, :], 1)
                pe.wait_ge(s_h, run(n) + N_CHUNKS)
                pe.wait_ge(s_hT, run(n, 1) + N_CHUNKS)
                transposes(e_tr_ps, 0, TPG)
                filters(place, 0, 2, 1)
                pe.wait_ge(s_hT, run(n) + N_CHUNKS)
                pe.wait_ge(s_mid, run(mlp, 1))
                pe.matmul(e_l1_ps, w["aw1_s"][:, :], hT[:, 0:GC], start=True, stop=True).then_inc(s_l1, 1)
                pe.wait_ge(s_mid, run(mlp))
                pe.wait_ge(s_res, run(mlp, 1))
                layer2(e_l2_ps, TPG, w["aw2_s"][:, :], s_l2)
                window(place, 0, 2, 0, 1)

            def e_attr_loads(n, r):
                if isinstance(n, int):
                    return 16 * (LEGS + 1 + r // 2)
                return (n - r) * (16 // LEG_EARLY) + 16

            def output(place, c, mlp):
                pe.wait_ge(win_added, done(place, 0, 1))
                pe.wait_ge(s_mid, run(mlp, 1))
                layer1(lambda a, b: agg[:, bass.ds(c * CHC + a, b - a)], w["ow1_s"][:, :], s_l1)
                pe.wait_ge(s_mid, run(mlp))
                pe.wait_ge(s_res, run(mlp, 1))
                layer2(l2_ps, CH, w["ow2_s"][:, :], s_l2)
                pe.wait_ge(s_res, run(mlp))

            main_part(pe, turn, early, output, lambda: None)
            n = edges_left(pe)
            with pe.If(n > 0):
                with pe.Fori(0, EDGE_TILES) as t:
                    pe.wait_ge(r_in, t * 32 + 32)
                    pe.matmul(hid_ps[0][:, 0:P], w["fw1_s"][:, :], attr[:, 0:P], start=True, stop=True)\
                        .then_inc(r_l1, 1)
                    pe.wait_ge(r_hid, t + 1)
                    pe.wait_ge(r_msg, t + 1)
                    pe.matmul(fil_ps[0][:, 0:P], hid[:, 0, 0:P], w["fw2_s"][:, :], start=True, stop=False)
                    pe.matmul(fil_ps[0][:, 0:P], ones_b[:, :], fb2_rows[:, 0, :], start=False, stop=True)\
                        .then_inc(r_fil, 1)
                    for k in range(R_WINDOWS):
                        pe.wait_ge(r_one, t * R_WINDOWS + (k + 1))
                        pe.matmul(sum_ps[0], msg[:, 0, 0:P], r_onehot, start=True, stop=True).then_inc(r_win, 1)
                pe.wait_ge(r_add, EDGE_TILES * R_WINDOWS)
                with pe.Fori(0, N_CHUNKS - 1) as c:
                    pe.wait_ge(a_mid, run(c, 1))
                    layer1(lambda a, b: agg[:, bass.ds(c * CHC + a, b - a)], w["ow1_s"][:, :], a_l1)
                    pe.wait_ge(a_mid, run(c))
                    pe.wait_ge(a_res, run(c, 1))
                    layer2(l2_ps, CH, w["ow2_s"][:, :], a_l2)
                pe.wait_ge(a_res, run(N_CHUNKS - 2))
            output(GROUPS, N_CHUNKS - 1, LAST_MLP)


_W = ["fw1", "fb1", "fw2", "fb2", "aw1", "ab1", "aw2", "ab2", "ow1", "ob1", "ow2", "ob2"]


def kernel(x, src, dst, edge_attr_50, **weights):
    import concourse.bacc as bacc
    from concourse.bass_utils import run_bass_kernel_spmd

    pad = EDGE_TILES * P - N_EDGES
    src_p = np.concatenate([np.asarray(src), np.zeros(pad, np.asarray(src).dtype)])
    dst_p = np.concatenate([np.asarray(dst), np.full(pad, N_NODES, np.asarray(dst).dtype)])
    attr = np.zeros((NG, EDGE_TILES * P), np.asarray(edge_attr_50).dtype)
    attr[:, :N_EDGES] = np.asarray(edge_attr_50).T
    xp = np.zeros((NODE_TILES * P, F), np.asarray(x).dtype)
    xp[:N_NODES] = np.asarray(x)
    arrays = {
        "x": xp,
        "src": np.ascontiguousarray(src_p.reshape(TURNS + 1, TT, P).transpose(0, 2, 1)),
        "dst": np.ascontiguousarray(dst_p.reshape(EDGE_TILES, P).T),
        "attr": attr,
    }
    for n in _W:
        arrays[n] = np.ascontiguousarray(np.asarray(weights["L0_gnn_" + n]))

    nc = bacc.Bacc("TRN2", target_bir_lowering=False, num_devices=1)
    args = [nc.dram_tensor("in_" + n, a.shape, mybir.dt.from_np(a.dtype), kind="ExternalInput").ap()
            for n, a in arrays.items()]
    out = nc.dram_tensor("out", (NODE_TILES * P, F), mybir.dt.float32, kind="ExternalOutput").ap()
    gnn_layer(nc, *args, out)
    r = run_bass_kernel_spmd(nc, [{"in_" + n: a for n, a in arrays.items()}], core_ids=[0])
    return r.results[0]["out"][:N_NODES]
```

```python
import numpy as np
import concourse.bass as bass
from concourse import mybir
from contextlib import ExitStack

P = 128
F = 128
NG = 50
N_NODES = 6250
N_EDGES = 206250
NODE_TILES = -(-N_NODES // P)
CH = 7
N_CHUNKS = NODE_TILES // CH
CHC = CH * P
STAT_PARTS = ((0, 3), (3, N_CHUNKS))
TPG = 4
GC = TPG * P
EDGE_TILES = -(-N_EDGES // GC) * TPG
GROUPS = EDGE_TILES // TPG
SLOTS = 13
TT = SLOTS * TPG
TURNS = GROUPS // SLOTS - 1
EARLY = TURNS * TT
SLOTS_A = 7
PARTS = ((0, SLOTS_A), (SLOTS_A, SLOTS))
WIN = 64
RW = 512
R_WINDOWS = -(-(N_NODES + 1) // RW)
AGG = max(R_WINDOWS * RW, N_NODES + WIN)
EPS = 1e-5
assert NODE_TILES == N_CHUNKS * CH and GROUPS == (TURNS + 1) * SLOTS

LEGS, LEG_TURNS, LEG_EARLY = N_CHUNKS - 2, 5, 2
LEG_GROUPS = LEG_TURNS * SLOTS + LEG_EARLY
REST_TURNS = SLOTS - 1 - LEGS * LEG_EARLY
LAST_TURNS = TURNS - LEGS * LEG_TURNS - REST_TURNS
LAST_OUT = 4
REST_OUT = NODE_TILES - LEGS * CH - LAST_TURNS * LAST_OUT
assert REST_TURNS > 0 and LAST_TURNS > 0 and 0 < REST_OUT <= CH
OUTPUTS = LEGS + 1 + LAST_TURNS
CHECKPOINTS = [((c + 1) * LEG_TURNS * TT, (c + 1) * CHC) for c in range(LEGS)] + \
    [((TURNS - LAST_TURNS + t) * TT, (LEGS * CH + REST_OUT + t * LAST_OUT) * P) for t in range(LAST_TURNS)]


def main_part(eng, turn, early, output):
    early(0, 0, 1, 0, N_CHUNKS)
    with eng.Fori(0, LEGS) as leg:
        with eng.Fori(0, LEG_TURNS) as t:
            turn(leg * LEG_GROUPS + (t * SLOTS + 1), leg * LEG_TURNS + t)
        mlp = leg * (LEG_EARLY + 1) + (N_CHUNKS + 1)
        early(leg * LEG_GROUPS + (LEG_TURNS * SLOTS + 1), leg * LEG_EARLY + 1, LEG_EARLY, leg + 1, mlp)
        output(leg * LEG_GROUPS + (LEG_GROUPS + 1), leg * CH, CH, leg, mlp + LEG_EARLY)
    at, mlp = LEGS * LEG_GROUPS + 1, N_CHUNKS + 1 + LEGS * (LEG_EARLY + 1)
    with eng.Fori(0, REST_TURNS) as t:
        turn(t * (SLOTS + 1) + at, t + LEGS * LEG_TURNS)
        early(t * (SLOTS + 1) + (at + SLOTS), t + (LEGS * LEG_EARLY + 1), 1, t + (LEGS + 1), t + mlp)
    at += REST_TURNS * (SLOTS + 1)
    mlp += REST_TURNS
    output(at, LEGS * CH, REST_OUT, LEGS, mlp)
    with eng.Fori(0, LAST_TURNS) as t:
        turn(t * SLOTS + at, t + (TURNS - LAST_TURNS))
        output(t * SLOTS + (at + SLOTS), t * LAST_OUT + (LEGS * CH + REST_OUT), LAST_OUT, t + (LEGS + 1),
               t + (mlp + 1))


RING3 = [s % 2 for s in range(SLOTS - 1)] + [2]
RING2 = [s % 2 for s in range(SLOTS)]


def back(ring, s):
    return next(d for d in range(1, SLOTS + 1) if ring[(s - d) % SLOTS] == ring[s])


def done(place, s=0, d=0):
    return place + (SLOTS + 1 + s - d)


def run(c, d=0):
    return c + (3 - d)


def gnn_layer(nc, x, src_t, dst_t, attr_t, fw1, fb1, fw2, fb2, aw1, ab1, aw2, ab2, ow1, ob1, ow2, ob2, out):
    f32, i32, bf16 = mybir.dt.float32, mybir.dt.int32, mybir.dt.bfloat16
    ALU, ACT, AX = mybir.AluOpType, mybir.ActivationFunctionType, mybir.AxisListType

    table = nc.dram_tensor("node_table", [NODE_TILES * P, F], f32).ap()
    x_tiles = x.rearrange("(t p) f -> p t f", p=P)
    out_tiles = out.rearrange("(t p) f -> p t f", p=P)
    table_tiles = table.rearrange("(t p) f -> p t f", p=P)

    with ExitStack() as ctx:
        def sb(name, shape, dt=f32):
            return ctx.enter_context(nc.sbuf_tensor(name, shape, dt))

        def sem(name):
            return ctx.enter_context(nc.semaphore(name))

        ident = sb("ident", [P, P])
        ones = sb("ones", [P, P])
        ones_b = sb("ones_b", [P, P], bf16)
        iota = sb("iota", [P, RW])
        w = {n: sb(n, [a.shape[0], F]) for n, a in
             (("fw1_s", fw1), ("fw2_s", fw2), ("aw1_s", aw1), ("aw2_s", aw2), ("ow1_s", ow1), ("ow2_s", ow2))}
        cols = sb("cols", [P, 3])
        rows = sb("rows", [P, 3, F])
        fb2_part = sb("fb2_part", [P, 3, F], bf16)
        fb2_rest = sb("fb2_rest", [P, 2, F])
        fb2_rows = sb("fb2_rows", [P, TPG, F], bf16)
        xs = sb("xs", [P, NODE_TILES, F])
        hs = sb("hs", [P, 2, CH, F])
        hT = sb("hT", [P, CHC])
        mid = sb("mid", [P, CHC])
        res = sb("res", [P, CH, F])
        stats = sb("stats", [P, TT, 6])
        moments = sb("moments", [P, 4, NODE_TILES])
        dst_i = sb("dst_i", [P, EDGE_TILES], i32)
        first_dst = sb("first_dst", [1, GROUPS])
        rel = sb("rel", [P, EDGE_TILES])
        cover = sb("cover", [P, EDGE_TILES], bf16)
        in_order = sb("in_order", [P, EDGE_TILES], bf16)
        n_well = sb("n_well", [P, 1])
        n_left = sb("n_left", [P, 1], i32)
        agg = sb("agg", [P, AGG])
        src_ab = [sb("src_a", [P, SLOTS_A * TPG], i32), sb("src_b", [P, (SLOTS - SLOTS_A) * TPG], i32)]
        attr = sb("attr", [NG, SLOTS * GC])
        xg = sb("xg", [P, SLOTS, GC])
        hid = sb("hid", [P, 3, GC])
        msg = sb("msg", [P, 3, GC])
        onehot = sb("onehot", [P, 3, TPG, WIN])
        e_src = sb("e_src", [P, TT], i32)
        e_x = sb("e_x", [P, TT, F])
        e_moments = sb("e_moments", [P, 4, TT])
        e_attr = sb("e_attr", [NG, LEG_EARLY, GC])
        e_row = sb("e_row", [P, GC])
        warm = sb("warm", [P, 1])
        r_src = src_ab[0][:, 0:1]
        r_onehot = msg[:, 1, :]
        r_dst = xg[:, 1:5, :].rearrange("p s c -> p (s c)")[:, 0:EDGE_TILES]

        banks = [ctx.enter_context(nc.psum_tensor(f"banks{i}", [P, 1024], f32)) for i in range(4)]
        bank = [banks[i // 2][:, 512 * (i % 2):512 * (i % 2) + 512] for i in range(8)]
        hid_ps, fil_ps, sum_ps = bank[0:3], bank[3:6], bank[6:8]
        l1_ps, tr_ps, l2_ps, misc_ps = banks
        left_ps = sum_ps[1][:, 0:1]
        e_l1_ps, e_tr_ps, e_l2_ps = bank[0], bank[3], bank[4]

        s_node_wts, s_wts, s_cols, s_rows, s_dst = (sem(n) for n in ("s_node_wts", "s_wts", "s_cols", "s_rows", "s_dst"))
        s_x = [sem(f"s_x{i}") for i in range(N_CHUNKS)]
        s_pool, s_set, s_base, s_rel, s_cover, s_left = (
            sem(n) for n in ("s_pool", "s_set", "s_base", "s_rel", "s_cover", "s_left"))
        s_fb2, s_step, s_var, s_std, s_rstd = (sem(n) for n in ("s_fb2", "s_step", "s_var", "s_std", "s_rstd"))
        s_h, s_hx, s_tr, s_hT, s_l1, s_mid, s_l2, s_res = (
            sem(n) for n in ("s_h", "s_hx", "s_tr", "s_hT", "s_l1", "s_mid", "s_l2", "s_res"))
        s_tab, s_out, s_xs = sem("s_tab"), sem("s_out"), sem("s_xs")
        attr_in, src_in = [sem("attr_in_a"), sem("attr_in_b")], [sem("src_in_a"), sem("src_in_b")]
        gathered = [sem(f"gathered{s}") for s in range(SLOTS)]
        slot_taken, hid_sum, hid_done, fil_done, msg_done, win_done, win_added = (
            sem(n) for n in ("slot_taken", "hid_sum", "hid_done", "fil_done", "msg_done", "win_done", "win_added"))
        e_src_in = sem("e_src_in")
        e_attr_in = [sem(f"e_attr_in{r}") for r in range(LEG_EARLY)]
        r_key, r_in, r_gat, r_l1, r_hid, r_fil, r_msg, r_one, r_win, r_add = (
            sem(n) for n in ("r_key", "r_in", "r_gat", "r_l1", "r_hid", "r_fil", "r_msg", "r_one", "r_win", "r_add"))
        a_l1, a_mid, a_l2, a_res, a_out = (sem(n) for n in ("a_l1", "a_mid", "a_l2", "a_res", "a_out"))

        def edges_left(eng):
            eng.wait_ge(s_left, 1)
            return eng.value_load(n_left[0:1, 0:1], min_val=0, max_val=EDGE_TILES * P)

        block = ctx.enter_context(nc.Block())

        @block.sync
        def _(sp):
            sp.dma_start(e_src[:, :], src_t[TURNS, :, :]).then_inc(e_src_in, 16)
            for c in range(N_CHUNKS):
                sp.dma_start(xs[:, c * CH:(c + 1) * CH, :], x_tiles[:, c * CH:(c + 1) * CH, :]).then_inc(s_x[c], 16)
            sp.dma_start(dst_i[:, :], dst_t).then_inc(s_dst, 16)
            for name, a in (("fw1_s", fw1), ("fw2_s", fw2), ("ow1_s", ow1), ("ow2_s", ow2)):
                sp.dma_start(w[name][:, :], a).then_inc(s_wts, 16)
            sp.sem_inc(s_tab, 32)
            with sp.Fori(0, N_CHUNKS) as c:
                sp.wait_ge(s_res, run(c))
                sp.dma_start(table_tiles[:, bass.ds(c * CH, CH), :], res[:, :, :]).then_inc(s_tab, 16)

            def turn(place, n):
                for k, (a, b) in enumerate(PARTS):
                    for s in range(a, b):
                        sp.wait_ge(gathered[s], n * (16 * TPG) + 16 * TPG)
                    sp.dma_start(src_ab[k][:, :], src_t[bass.ds(n, 1), :, a * TPG:b * TPG]
                                 .rearrange("o p j -> p (o j)")).then_inc(src_in[k], 16)
                    sp.wait_ge(hid_sum, done(place, b - 1, SLOTS))
                    sp.dma_start(attr[:, a * GC:b * GC], attr_t[:, bass.ds(n * (SLOTS * GC) + a * GC, (b - a) * GC)])\
                        .then_inc(attr_in[k], 16)

            def early(place, n, count, before, mlp):
                sp.wait_ge(hid_sum, done(place, 0, SLOTS))
                for r in range(count):
                    sp.dma_start(e_attr[:, r, :], attr_t[:, bass.ds(n * GC + (EARLY * P + r * GC), GC)])\
                        .then_inc(e_attr_in[r], 16)

            main_part(sp, turn, early, lambda *_: None)
            n = edges_left(sp)
            with sp.If(n > 0):
                with sp.Fori(0, TURNS + 1) as turn:
                    with sp.Fori(0, TT) as j:
                        t = turn * TT + j
                        sp.wait_ge(r_msg, t + 1)
                        sp.dma_start(r_src, src_t[bass.ds(turn, 1), :, bass.ds(j, 1)].rearrange("o p j -> p (o j)"),
                                     allow_slow_non_contiguous=True).then_inc(r_in, 16)
                        sp.dma_start(attr[:, 0:P], attr_t[:, bass.ds(t * P, P)]).then_inc(r_in, 16)

        @block.gpsimd
        def _(pool):
            pool.memset(ident[:, :], 0.0).then_inc(s_pool, 1)
            pool.iota(iota[:, :], pattern=[[1, RW]], base=0, channel_multiplier=0,
                      allow_small_or_imprecise_dtypes=True).then_inc(s_pool, 1)
            pool.wait_ge(s_pool, 2)
            pool.affine_select(out=ident[:, :], in_=ident[:, :], compare_op=ALU.not_equal, fill=1.0, base=0,
                               pattern=[[-1, P]], channel_multiplier=1).then_inc(s_pool, 1)
            pool.wait_ge(s_pool, 3)
            pool.wait_ge(e_src_in, 16)
            for j in range(TT):
                pool.indirect_dma_start(e_x[:, j, :], None, x[:, :],
                                        bass.IndirectOffsetOnAxis(ap=e_src[:, j:j + 1], axis=0)).then_inc(gathered[j // TPG], 16)
            pool.wait_ge(s_tab, 16 * run(N_CHUNKS - 1))

            def turn(place, n):
                for s in range(SLOTS):
                    k = s // SLOTS_A
                    if s in (0, SLOTS_A):
                        pool.wait_ge(src_in[k], n * 16 + 16)
                    pool.wait_ge(msg_done, done(place, s, SLOTS))
                    pool.sem_inc(slot_taken, 1)
                    for j in range(TPG):
                        col = (s - k * SLOTS_A) * TPG + j
                        pool.indirect_dma_start(xg[:, s, j * P:(j + 1) * P], None, table[:, :],
                                                bass.IndirectOffsetOnAxis(ap=src_ab[k][:, col:col + 1], axis=0))\
                            .then_inc(gathered[s], 16)

            main_part(pool, turn, lambda *_: None, lambda *_: None)
            n = edges_left(pool)
            with pool.If(n > 0):
                with pool.Fori(0, EDGE_TILES) as t:
                    pool.wait_ge(r_in, t * 32 + 32)
                    pool.wait_ge(r_msg, t + 1)
                    pool.sem_inc(slot_taken, 1)
                    pool.indirect_dma_start(xg[:, 0, 0:P], None, table[:, :],
                                            bass.IndirectOffsetOnAxis(ap=r_src, axis=0)).then_inc(r_gat, 16)

        @block.scalar
        def _(act):
            for name, a in (("aw1_s", aw1), ("aw2_s", aw2)):
                act.dma_start(w[name][:, :], a).then_inc(s_node_wts, 16)
            for i, b in enumerate((fb2, ab2, ob2)):
                act.dma_start(rows[:, i, :], b.rearrange("(o f) -> o f", o=1).to_broadcast([P, F])).then_inc(s_rows, 16)
            for i, b in enumerate((fb1, ab1, ob1)):
                act.dma_start(cols[:, i:i + 1], b.rearrange("(f o) -> f o", o=1)).then_inc(s_cols, 16)
            for ahead in (s_h, s_mid, a_mid):
                act.sem_inc(ahead, 2)
            act.sem_inc(s_out, 32)
            act.sem_inc(a_out, 32)
            act.sem_inc(hid_done, SLOTS)

            def deviations(k):
                act.wait_ge(s_var, k + 1)
                m = moments[:, 2, STAT_PARTS[k][0] * CH:STAT_PARTS[k][1] * CH]
                act.activation(m, m, ACT.Sqrt).then_inc(s_std, 1)

            def relu_ln(c, b):
                act.wait_ge(s_tr, run(c, 2))
                act.wait_ge(s_hx, run(c, 2))
                for j in range(CH):
                    t = c * CH + j
                    i = act.activation(hs[:, b, j, :], xs[:, bass.ds(t, 1), :].rearrange("p o f -> p (o f)"), ACT.Relu,
                                       bias=moments[:, 3, bass.ds(t, 1)], scale=moments[:, 2, bass.ds(t, 1)])
                i.then_inc(s_h, 1)

            def silu_mid(mlp, n, bias, summed=s_l1, used=s_l2, mid_done=s_mid):
                act.wait_ge(summed, run(mlp))
                act.wait_ge(used, run(mlp, 1))
                act.activation(mid[:, 0:n], l1_ps[:, 0:n], ACT.Silu, bias=cols[:, bias:bias + 1]).then_inc(mid_done, 1)

            act.wait_ge(s_set, 1)
            act.activation(warm[:, :], ones[:, 0:1], ACT.Sqrt)
            deviations(0)
            act.wait_ge(s_rstd, 1)
            relu_ln(0, 0)
            relu_ln(1, 1)
            deviations(1)
            act.wait_ge(s_cols, 48)
            act.activation(warm[:, :], cols[:, 0:1], ACT.Silu)
            act.wait_ge(s_rstd, 2)
            with act.Fori(0, N_CHUNKS // 2 - 1) as pair:
                for k in range(2):
                    silu_mid(2 * pair + k, CHC, 1)
                    relu_ln(2 * pair + (k + 2), k)
            silu_mid(N_CHUNKS - 3, CHC, 1)
            relu_ln(N_CHUNKS - 1, 0)
            silu_mid(N_CHUNKS - 2, CHC, 1)
            silu_mid(N_CHUNKS - 1, CHC, 1)
            act.wait_ge(s_var, 3)
            act.activation(e_moments[:, 2, :], e_moments[:, 2, :], ACT.Sqrt).then_inc(s_std, 1)

            def silu_hid(place, s, b, d):
                act.wait_ge(hid_sum, done(place, s))
                act.wait_ge(fil_done, done(place, s, d))
                act.activation(hid[:, b, :], hid_ps[b], ACT.Silu, bias=cols[:, 0:1]).then_inc(hid_done, 1)

            def turn(place, n):
                for s in range(SLOTS):
                    silu_hid(place, s, RING3[s], back(RING3, s))

            def relu_early(n, r):
                act.wait_ge(s_tr, run(n, 1 if r == 0 else 2) + N_CHUNKS)
                for j in range(TPG):
                    t = n * TPG + j
                    i = act.activation(hs[:, r % 2, j, :], e_x[:, bass.ds(t, 1), :].rearrange("p o f -> p (o f)"),
                                       ACT.Relu, bias=e_moments[:, 3, bass.ds(t, 1)],
                                       scale=e_moments[:, 2, bass.ds(t, 1)])
                i.then_inc(s_h, 1)

            def early(place, n, count, before, mlp):
                act.wait_ge(s_rstd, 3)
                relu_early(n, 0)
                silu_hid(place, 0, 2, 1)
                for r in range(count):
                    if r + 1 < count:
                        relu_early(n + (r + 1), r + 1)
                    silu_mid(mlp + r, GC, 1)
                    if r + 1 < count:
                        silu_hid(place, r + 1, 2, 1)

            def output(place, first, n, before, mlp):
                silu_mid(mlp, n * P, 2)
                act.wait_ge(s_res, run(mlp))
                act.dma_start(out_tiles[:, bass.ds(first, n), :], res[:, 0:n, :]).then_inc(s_out, 16)

            act.wait_ge(s_hx, run(N_CHUNKS - 1))
            main_part(act, turn, early, output)
            act.wait_ge(s_out, 16 * run(OUTPUTS - 1))
            n = edges_left(act)
            with act.If(n > 0):
                with act.Fori(0, EDGE_TILES) as t:
                    act.wait_ge(r_l1, t + 1)
                    act.activation(hid[:, 0, 0:P], hid_ps[0][:, 0:P], ACT.Silu, bias=cols[:, 0:1]).then_inc(r_hid, 1)
                with act.Fori(0, N_CHUNKS) as c:
                    silu_mid(c, CHC, 2, a_l1, a_l2, a_mid)
                    act.wait_ge(a_res, run(c))
                    act.dma_start(out_tiles[:, bass.ds(c * CH, CH), :], res[:, :, :]).then_inc(a_out, 16)
                act.wait_ge(a_out, 16 * run(N_CHUNKS - 1))

        @block.vector
        def _(dve):
            for ahead in (s_hT, s_hx, s_res, a_res):
                dve.sem_inc(ahead, 2)
            dve.sem_inc(msg_done, SLOTS)
            dve.sem_inc(win_added, SLOTS)

            step = [0]

            def moments_of(st, m):
                def link(i):
                    step[0] += 1
                    i.then_inc(s_step, 1)
                    dve.wait_ge(s_step, step[0])

                link(dve.tensor_tensor(m[:, 0, :], st[:, :, 1], st[:, :, 4], ALU.add))
                link(dve.tensor_tensor(m[:, 1, :], st[:, :, 1], st[:, :, 4], ALU.subtract))
                link(dve.tensor_tensor(m[:, 2, :], st[:, :, 2], st[:, :, 5], ALU.add))
                link(dve.tensor_tensor(m[:, 1, :], m[:, 1, :], m[:, 1, :], ALU.mult))
                link(dve.scalar_tensor_tensor(out=m[:, 2, :], in0=m[:, 1, :], scalar=F / 4.0, in1=m[:, 2, :],
                                              op0=ALU.mult, op1=ALU.add))
                dve.tensor_scalar(m[:, 2, :], m[:, 2, :], 1.0 / F, EPS, ALU.mult, ALU.add).then_inc(s_var, 1)

            def scales_of(m, n_std):
                dve.wait_ge(s_std, n_std)
                dve.reciprocal(m[:, 2, :], m[:, 2, :]).then_inc(s_step, 1)
                step[0] += 1
                dve.wait_ge(s_step, step[0])
                dve.scalar_tensor_tensor(out=m[:, 3, :], in0=m[:, 0, :], scalar=-0.5, in1=m[:, 2, :],
                                         op0=ALU.mult, op1=ALU.mult).then_inc(s_rstd, 1)

            def transposed(c):
                dve.wait_ge(s_tr, run(c))
                dve.wait_ge(s_l1, run(c, 1))
                dve.tensor_copy(hT[:, :], tr_ps[:, 0:CHC]).then_inc(s_hT, 1)

            def add_h(c, b):
                dve.wait_ge(s_h, run(c))
                xc = xs[:, bass.ds(c * CH, CH), :]
                dve.tensor_tensor(xc, xc, hs[:, b, :, :], ALU.add).then_inc(s_hx, 1)

            dve.memset(ones[:, :], 1.0)
            dve.memset(ones_b[:, :], 1.0)
            dve.memset(fb2_rows[:, :, :], 0.0)
            dve.memset(in_order[:, 0:CHECKPOINTS[0][0]], 0.0)
            for (a, least), (b, _) in zip(CHECKPOINTS, CHECKPOINTS[1:] + [(EDGE_TILES, 0)]):
                i = dve.memset(in_order[:, a:b], float(least))
            i.then_inc(s_set, 1)

            for k, (first, last) in enumerate(STAT_PARTS):
                for c in range(first, last):
                    dve.wait_ge(s_x[c], 16)
                    for t in range(c * CH, (c + 1) * CH):
                        i = dve.bn_stats(stats[:, t, :], xs[:, t, :])
                i.then_inc(s_step, 1)
                step[0] += 1
                if k == 1:
                    transposed(0)
                dve.wait_ge(s_step, step[0])
                part = moments[:, :, first * CH:last * CH]
                moments_of(stats[:, first * CH:last * CH, :], part)
                scales_of(part, k + 1)

            def add_bias(c):
                dve.wait_ge(s_l2, run(c))
                dve.wait_ge(s_tab, run(c, 1) * 16)
                dve.tensor_tensor(res[:, :, :], l2_ps[:, 0:CHC].rearrange("p (t f) -> p t f", f=F),
                                  rows[:, 1:2, :].to_broadcast([P, CH, F]), ALU.add).then_inc(s_res, 1)

            dve.wait_ge(s_rows, 48)
            add_h(0, 0)
            with dve.Fori(0, (N_CHUNKS - 1) // 2) as pair:
                for k in range(2):
                    transposed(2 * pair + (k + 1))
                    add_h(2 * pair + (k + 1), (k + 1) % 2)
                    add_bias(2 * pair + k)
            add_bias(N_CHUNKS - 1)

            dve.memset(agg[:, :], 0.0).then_inc(s_set, 1)

            dve.wait_ge(s_dst, 16)
            dve.tensor_copy(first_dst[:, :], dst_i[0:1, :].rearrange("p (g j) -> p g j", j=TPG)[:, :, 0]).then_inc(s_rel, 1)
            dve.tensor_copy(fb2_part[:, 0, :], rows[:, 0, :]).then_inc(s_fb2, 1)
            dve.wait_ge(s_fb2, 1)
            dve.tensor_tensor(fb2_rest[:, 0, :], rows[:, 0, :], fb2_part[:, 0, :], ALU.subtract).then_inc(s_fb2, 1)
            dve.wait_ge(s_fb2, 2)
            dve.tensor_copy(fb2_part[:, 1, :], fb2_rest[:, 0, :]).then_inc(s_fb2, 1)
            dve.wait_ge(s_fb2, 3)
            dve.tensor_tensor(fb2_rest[:, 1, :], fb2_rest[:, 0, :], fb2_part[:, 1, :], ALU.subtract).then_inc(s_fb2, 1)
            dve.wait_ge(s_fb2, 4)
            dve.tensor_copy(fb2_part[:, 2, :], fb2_rest[:, 1, :]).then_inc(s_fb2, 1)
            dve.wait_ge(s_fb2, 5)
            dve.wait_ge(s_set, 1)
            for i in range(3):
                dve.tensor_copy(fb2_rows[32 * i:32 * i + 1, :, :],
                                fb2_part[32 * i:32 * i + 1, i:i + 1, :].to_broadcast([1, TPG, F])).then_inc(s_fb2, 1)

            dve.wait_ge(s_base, 1)
            dve.tensor_tensor(rel[:, :].rearrange("p (g j) -> p g j", j=TPG),
                              dst_i[:, :].rearrange("p (g j) -> p g j", j=TPG),
                              misc_ps[:, 0:GROUPS].rearrange("p (g o) -> p g o", o=1).to_broadcast([P, GROUPS, TPG]),
                              ALU.subtract).then_inc(s_rel, 1)

            dve.wait_ge(s_rel, 2)
            dve.tensor_scalar(cover[:, :], rel[:, :], 0.0, None, ALU.is_ge).then_inc(s_cover, 1)
            dve.wait_ge(s_cover, 1)
            dve.scalar_tensor_tensor(out=cover[:, :], in0=rel[:, :], scalar=float(WIN), in1=cover[:, :],
                                     op0=ALU.is_lt, op1=ALU.mult).then_inc(s_cover, 1)
            dve.tensor_tensor(in_order[:, :], dst_i[:, :], in_order[:, :], ALU.is_ge).then_inc(s_cover, 1)
            dve.wait_ge(s_cover, 3)
            dve.tensor_tensor(in_order[:, :], in_order[:, :], cover[:, :], ALU.mult).then_inc(s_cover, 1)
            dve.wait_ge(s_cover, 4)
            dve.reduce_sum(n_well[:, :], in_order[:, :], AX.X).then_inc(s_cover, 1)
            dve.wait_ge(s_cover, 6)
            dve.tensor_scalar(n_left[:, :], left_ps, -1.0, float(EDGE_TILES * P), ALU.mult,
                              ALU.add).then_inc(s_left, 1)

            for t in range(TT):
                if t % TPG == 0:
                    dve.wait_ge(gathered[t // TPG], 16 * TPG)
                i = dve.bn_stats(stats[:, t, :], e_x[:, t, :])
            i.then_inc(s_step, 1)
            step[0] += 1
            dve.wait_ge(s_step, step[0])
            moments_of(stats, e_moments)
            scales_of(e_moments, 3)

            dve.wait_ge(s_hx, run(N_CHUNKS - 1))
            dve.wait_ge(s_pool, 3)
            dve.wait_ge(s_set, 2)
            dve.wait_ge(s_tab, 16 * run(N_CHUNKS - 1))

            def one_hot(place, s, b, tile, d):
                dve.wait_ge(win_done, done(place, s, d))
                r = rel[:, bass.ds(tile, TPG)].rearrange("p (j o) -> p j o", o=1)
                dve.tensor_tensor(onehot[:, b, :, :],
                                  iota[:, 0:WIN].rearrange("p (o k) -> p o k", o=1).to_broadcast([P, TPG, WIN]),
                                  r.to_broadcast([P, TPG, WIN]), ALU.is_equal)

            def add_window(place, s, k, tile):
                base = dve.value_load(dst_i[0:1, bass.ds(tile, 1)], min_val=0, max_val=N_NODES)
                dve.wait_ge(win_done, done(place, s))
                dve.wait_ge(win_added, done(place, s, 1))
                window = agg[:, bass.ds(base, WIN)]
                dve.tensor_tensor(window, window, sum_ps[k][:, 0:WIN], ALU.add).then_inc(win_added, 1)

            def turn(place, n):
                for s in range(SLOTS):
                    b = RING3[s]
                    one_hot(place, s, b, n * TT + s * TPG, back(RING3, s))
                    dve.wait_ge(gathered[s], n * (16 * TPG) + 32 * TPG)
                    dve.wait_ge(fil_done, done(place, s))
                    dve.tensor_tensor(msg[:, b, :], fil_ps[b], xg[:, s, :], ALU.mult).then_inc(msg_done, 1)
                    if s > 0:
                        add_window(place, s - 1, RING2[s - 1], n * TT + (s - 1) * TPG)
                add_window(place, SLOTS - 1, RING2[SLOTS - 1], n * TT + (SLOTS - 1) * TPG)

            def early_hT(n, mlp):
                dve.wait_ge(s_tr, run(n) + N_CHUNKS)
                dve.wait_ge(s_l1, run(mlp, 1))
                dve.tensor_copy(hT[:, 0:GC], e_tr_ps).then_inc(s_hT, 1)

            def early(place, n, count, before, mlp):
                early_hT(n, mlp)
                for r in range(count):
                    tile = n * TPG + (EARLY + r * TPG)
                    one_hot(place, r, 2, tile, 1)
                    if r + 1 < count:
                        early_hT(n + (r + 1), mlp + (r + 1))
                    dve.wait_ge(s_l2, run(mlp + r))
                    dve.tensor_tensor(e_row[:, :].rearrange("p (j f) -> p j f", f=F),
                                      e_l2_ps.rearrange("p (j f) -> p j f", f=F),
                                      rows[:, 1:2, :].to_broadcast([P, TPG, F]), ALU.add).then_inc(s_res, 1)
                    dve.wait_ge(s_res, run(mlp + r))
                    dve.wait_ge(fil_done, done(place, r))
                    dve.tensor_tensor(msg[:, 2, :], fil_ps[2], e_row[:, :], ALU.mult).then_inc(msg_done, 1)
                    add_window(place, r, 0, tile)

            def output(place, first, n, before, mlp):
                xc = xs[:, bass.ds(first, n), :]
                dve.tensor_tensor(xc, xc, rows[:, 2:3, :].to_broadcast([P, n, F]), ALU.add).then_inc(s_xs, 1)
                dve.wait_ge(s_l2, run(mlp))
                dve.wait_ge(s_out, run(before, 1) * 16)
                dve.wait_ge(s_xs, before + 1)
                dve.tensor_tensor(res[:, 0:n, :], l2_ps[:, 0:n * P].rearrange("p (t f) -> p t f", f=F), xc,
                                  ALU.add).then_inc(s_res, 1)

            main_part(dve, turn, early, output)
            n = edges_left(dve)
            with dve.If(n > 0):
                dve.wait_ge(msg_done, done(GROUPS - 1))
                dve.tensor_scalar(r_dst, cover[:, :], float(-2 * AGG), None, ALU.mult).then_inc(r_key, 1)
                dve.wait_ge(r_key, 1)
                dve.tensor_tensor(r_dst, r_dst, dst_i[:, :], ALU.add).then_inc(r_key, 1)
                dve.wait_ge(r_key, 2)
                dve.wait_ge(win_added, done(GROUPS - 1))
                dve.sem_inc(r_msg, 1)
                dve.sem_inc(r_win, 1)
                with dve.Fori(0, EDGE_TILES) as t:
                    dve.wait_ge(r_gat, t * 16 + 16)
                    dve.wait_ge(r_fil, t + 1)
                    dve.wait_ge(r_win, t * R_WINDOWS + 1)
                    dve.tensor_tensor(msg[:, 0, 0:P], fil_ps[0][:, 0:P], xg[:, 0, 0:P], ALU.mult).then_inc(r_msg, 1)
                    for k in range(R_WINDOWS):
                        dve.wait_ge(r_win, t * R_WINDOWS + (k + 1))
                        dve.tensor_scalar(r_onehot, iota[:, :], float(k * RW), r_dst[:, bass.ds(t, 1)],
                                          ALU.add, ALU.is_equal).then_inc(r_one, 1)
                        dve.wait_ge(r_win, t * R_WINDOWS + (k + 2))
                        dve.tensor_tensor(agg[:, k * RW:(k + 1) * RW], agg[:, k * RW:(k + 1) * RW], sum_ps[0],
                                          ALU.add).then_inc(r_add, 1)
                        dve.wait_ge(r_add, t * R_WINDOWS + (k + 1))
                dve.wait_ge(s_out, 16 * run(OUTPUTS - 1))
                with dve.Fori(0, N_CHUNKS) as c:
                    dve.wait_ge(a_l2, run(c))
                    dve.wait_ge(a_out, run(c, 1) * 16)
                    dve.tensor_tensor(res[:, :, :], l2_ps[:, 0:CHC].rearrange("p (t f) -> p t f", f=F),
                                      xs[:, bass.ds(c * CH, CH), :], ALU.add).then_inc(a_res, 1)

        @block.tensor
        def _(pe):
            def transposes(to, b, n_tiles):
                for j in range(n_tiles):
                    i = pe.transpose(to[:, j * P:(j + 1) * P], hs[:, b, j, :], ident[:, :])
                i.then_inc(s_tr, 1)

            def layer1(src, n_tiles, weights, summed):
                for a in range(0, n_tiles * P, GC):
                    b = min(a + GC, n_tiles * P)
                    i = pe.matmul(l1_ps[:, a:b], weights, src(a, b), start=True, stop=True)
                i.then_inc(summed, 1)

            def layer2(to, n_tiles, weights, summed):
                for j in range(n_tiles):
                    i = pe.matmul(to[:, j * P:(j + 1) * P], mid[:, j * P:(j + 1) * P], weights, start=True, stop=True)
                i.then_inc(summed, 1)

            def node_transposes(c, b):
                pe.wait_ge(s_h, run(c))
                pe.wait_ge(s_hT, run(c, 1))
                transposes(tr_ps, b, CH)

            def node_layer1(c):
                pe.wait_ge(s_hT, run(c))
                pe.wait_ge(s_mid, run(c, 1))
                layer1(lambda a, b: hT[:, a:b], CH, w["aw1_s"][:, :], s_l1)

            def node_layer2(c):
                pe.wait_ge(s_mid, run(c))
                pe.wait_ge(s_res, run(c, 1))
                layer2(l2_ps, CH, w["aw2_s"][:, :], s_l2)

            for ahead in (s_tr, s_l1, s_l2, a_l1, a_l2):
                pe.sem_inc(ahead, 2)
            for ahead in (hid_sum, fil_done, win_done):
                pe.sem_inc(ahead, SLOTS)
            pe.wait_ge(s_pool, 3)
            pe.wait_ge(s_node_wts, 32)
            node_transposes(0, 0)
            with pe.Fori(0, (N_CHUNKS - 1) // 2) as pair:
                for k in range(2):
                    node_layer1(2 * pair + k)
                    node_transposes(2 * pair + (k + 1), (k + 1) % 2)
                    node_layer2(2 * pair + k)
            node_layer1(N_CHUNKS - 1)
            node_layer2(N_CHUNKS - 1)
            pe.wait_ge(s_set, 1)
            pe.wait_ge(s_rel, 1)
            pe.matmul(misc_ps[:, 0:GROUPS], ones[0:1, :], first_dst[:, :], start=True, stop=True).then_inc(s_base, 1)
            pe.wait_ge(s_rel, 2)
            pe.wait_ge(s_res, run(N_CHUNKS - 1))
            pe.wait_ge(s_fb2, 8)
            pe.wait_ge(s_wts, 64)
            pe.wait_ge(s_cover, 5)
            pe.matmul(left_ps, ones[:, :], n_well[:, :], start=True, stop=True).then_inc(s_cover, 1)
            pe.wait_ge(s_left, 1)

            def hidden(place, s, b, features, d):
                pe.wait_ge(hid_done, done(place, s, d))
                pe.matmul(hid_ps[b], w["fw1_s"][:, :], features, start=True, stop=True).then_inc(hid_sum, 1)

            def filters(place, s, b, d):
                pe.wait_ge(msg_done, done(place, s, d))
                pe.wait_ge(hid_done, done(place, s))
                for j in range(TPG):
                    pe.matmul(fil_ps[b][:, j * P:(j + 1) * P], hid[:, b, j * P:(j + 1) * P], w["fw2_s"][:, :],
                              start=(j == 0), stop=False)
                pe.matmul(fil_ps[b], ones_b[:, :], fb2_rows[:, :, :].rearrange("p j f -> p (j f)"), start=False,
                          stop=True).then_inc(fil_done, 1)

            def window(place, s, b, k, d):
                pe.wait_ge(win_added, done(place, s, d))
                pe.wait_ge(msg_done, done(place, s))
                for j in range(TPG):
                    i = pe.matmul(sum_ps[k][:, 0:WIN], msg[:, b, j * P:(j + 1) * P], onehot[:, b, j, :],
                                  start=(j == 0), stop=(j == TPG - 1))
                i.then_inc(win_done, 1)

            def turn_hidden(place, n, s):
                if s in (0, SLOTS_A):
                    pe.wait_ge(attr_in[s // SLOTS_A], n * 16 + 16)
                hidden(place, s, RING3[s], attr[:, s * GC:(s + 1) * GC], back(RING3, s))

            def turn(place, n):
                turn_hidden(place, n, 0)
                for s in range(SLOTS):
                    if s + 1 < SLOTS:
                        turn_hidden(place, n, s + 1)
                    filters(place, s, RING3[s], back(RING3, s))
                    if s > 0:
                        window(place, s - 1, RING3[s - 1], RING2[s - 1], back(RING2, s - 1))
                window(place, SLOTS - 1, RING3[SLOTS - 1], RING2[SLOTS - 1], back(RING2, SLOTS - 1))

            def early_start(place, n, r, before):
                pe.wait_ge(e_attr_in[r], (before - r) * 16 + 16)
                hidden(place, r, 2, e_attr[:, r, :], 1)
                pe.wait_ge(s_h, run(n + r) + N_CHUNKS)
                pe.wait_ge(s_hT, run(n + r, 1) + N_CHUNKS)
                transposes(e_tr_ps, r % 2, TPG)

            def early_layer1(n, mlp):
                pe.wait_ge(s_hT, run(n) + N_CHUNKS)
                pe.wait_ge(s_mid, run(mlp, 1))
                pe.matmul(e_l1_ps, w["aw1_s"][:, :], hT[:, 0:GC], start=True, stop=True).then_inc(s_l1, 1)

            def early(place, n, count, before, mlp):
                early_start(place, n, 0, before)
                early_layer1(n, mlp)
                for r in range(count):
                    filters(place, r, 2, 1)
                    if r + 1 < count:
                        early_start(place, n, r + 1, before)
                    pe.wait_ge(s_mid, run(mlp + r))
                    pe.wait_ge(s_res, run(mlp + r, 1))
                    layer2(e_l2_ps, TPG, w["aw2_s"][:, :], s_l2)
                    if r + 1 < count:
                        early_layer1(n + (r + 1), mlp + (r + 1))
                    window(place, r, 2, 0, 1)

            def output(place, first, n, before, mlp):
                pe.wait_ge(win_added, done(place, 0, 1))
                pe.wait_ge(s_mid, run(mlp, 1))
                layer1(lambda a, b: agg[:, bass.ds(first * P + a, b - a)], n, w["ow1_s"][:, :], s_l1)
                pe.wait_ge(s_mid, run(mlp))
                pe.wait_ge(s_res, run(mlp, 1))
                layer2(l2_ps, n, w["ow2_s"][:, :], s_l2)
                pe.wait_ge(s_res, run(mlp))

            main_part(pe, turn, early, output)
            n = edges_left(pe)
            with pe.If(n > 0):
                with pe.Fori(0, EDGE_TILES) as t:
                    pe.wait_ge(r_in, t * 32 + 32)
                    pe.matmul(hid_ps[0][:, 0:P], w["fw1_s"][:, :], attr[:, 0:P], start=True, stop=True)\
                        .then_inc(r_l1, 1)
                    pe.wait_ge(r_hid, t + 1)
                    pe.wait_ge(r_msg, t + 1)
                    pe.matmul(fil_ps[0][:, 0:P], hid[:, 0, 0:P], w["fw2_s"][:, :], start=True, stop=False)
                    pe.matmul(fil_ps[0][:, 0:P], ones_b[:, :], fb2_rows[:, 0, :], start=False, stop=True)\
                        .then_inc(r_fil, 1)
                    for k in range(R_WINDOWS):
                        pe.wait_ge(r_one, t * R_WINDOWS + (k + 1))
                        pe.matmul(sum_ps[0], msg[:, 0, 0:P], r_onehot, start=True, stop=True).then_inc(r_win, 1)
                pe.wait_ge(r_add, EDGE_TILES * R_WINDOWS)
                with pe.Fori(0, N_CHUNKS) as c:
                    pe.wait_ge(a_mid, run(c, 1))
                    layer1(lambda a, b: agg[:, bass.ds(c * CHC + a, b - a)], CH, w["ow1_s"][:, :], a_l1)
                    pe.wait_ge(a_mid, run(c))
                    pe.wait_ge(a_res, run(c, 1))
                    layer2(l2_ps, CH, w["ow2_s"][:, :], a_l2)


_W = ["fw1", "fb1", "fw2", "fb2", "aw1", "ab1", "aw2", "ab2", "ow1", "ob1", "ow2", "ob2"]


def kernel(x, src, dst, edge_attr_50, **weights):
    import concourse.bacc as bacc
    from concourse.bass_utils import run_bass_kernel_spmd

    pad = EDGE_TILES * P - N_EDGES
    src_p = np.concatenate([np.asarray(src), np.zeros(pad, np.asarray(src).dtype)])
    dst_p = np.concatenate([np.asarray(dst), np.full(pad, N_NODES, np.asarray(dst).dtype)])
    attr = np.zeros((NG, EDGE_TILES * P), np.asarray(edge_attr_50).dtype)
    attr[:, :N_EDGES] = np.asarray(edge_attr_50).T
    xp = np.zeros((NODE_TILES * P, F), np.asarray(x).dtype)
    xp[:N_NODES] = np.asarray(x)
    arrays = {
        "x": xp,
        "src": np.ascontiguousarray(src_p.reshape(TURNS + 1, TT, P).transpose(0, 2, 1)),
        "dst": np.ascontiguousarray(dst_p.reshape(EDGE_TILES, P).T),
        "attr": attr,
    }
    for n in _W:
        arrays[n] = np.ascontiguousarray(np.asarray(weights["L0_gnn_" + n]))

    nc = bacc.Bacc("TRN2", target_bir_lowering=False, num_devices=1)
    args = [nc.dram_tensor("in_" + n, a.shape, mybir.dt.from_np(a.dtype), kind="ExternalInput").ap()
            for n, a in arrays.items()]
    out = nc.dram_tensor("out", (NODE_TILES * P, F), mybir.dt.float32, kind="ExternalOutput").ap()
    gnn_layer(nc, *args, out)
    r = run_bass_kernel_spmd(nc, [{"in_" + n: a for n, a in arrays.items()}], core_ids=[0])
    return r.results[0]["out"][:N_NODES]
```
